# Optimizing a Trainium2 kernel written in Bass

```python
import numpy as np
import jax
import jax.numpy as jnp

def _softmax(x, axis=-1):
    return jax.nn.softmax(x, axis=axis)

def _gelu(x):
    return jax.nn.gelu(x, approximate=True)

def _silu(x):
    return jax.nn.silu(x)

def _sigmoid(x):
    return jax.nn.sigmoid(x)

def _layernorm(x, axis=-1, eps=1e-05):
    m = jnp.mean(x, axis=axis, keepdims=True)
    v = jnp.var(x, axis=axis, keepdims=True)
    return (x - m) / jnp.sqrt(v + eps)

def _scatter_add(tgt, idx, src, axis=0):
    return tgt.at[idx].add(src)

def _segment_sum(src, seg, n):
    return jax.ops.segment_sum(src, seg, n)
kernel_name = 'mk_decoder_preln_d1_seqx_r8_b86329'

def setup_inputs(seed: int=0):
    np.random.seed(seed)
    _w = jnp.asarray

    def _rec_inputs():
        import jax
        import jax.numpy as jnp
        _rk = jax.random.key(seed)
        x = -0.0002928 + 1 * jax.random.normal(jax.random.fold_in(_rk, 1), (32, 56, 128), jnp.float32)
        _lenS = 56 - jax.random.randint(jax.random.fold_in(_rk, 7), (32,), 0, max(1, 56 // 4) + 1, jnp.int32)
        _lenS2 = 1500 - jax.random.randint(jax.random.fold_in(_rk, 8), (32,), 0, max(1, 1500 // 4) + 1, jnp.int32)
        _ctx_1024P = jax.random.normal(jax.random.fold_in(_rk, 11), (32, 16, 128), jnp.float32)
        _ctx_1024c = jax.random.dirichlet(jax.random.fold_in(_rk, 511), 0.3 * jnp.ones((16,), jnp.float32), (32, 1500))
        _ctx_1024t = jnp.einsum('bsk,bkd->bsd', _ctx_1024c, _ctx_1024P)
        _ctx_1024t = _ctx_1024t * jax.lax.rsqrt(jnp.mean(jnp.square(_ctx_1024t)) + 1e-12) * 0.953939
        ctx_1024 = -1.39393e-06 + 0.999914 * (_ctx_1024t + 0.3 * jax.random.normal(jax.random.fold_in(_rk, 611), (32, 1500, 128), jnp.float32))
        _validS = jnp.arange(56)[None, :] < _lenS[:, None]
        _validS2 = jnp.arange(1500)[None, :] < _lenS2[:, None]
        _causal = jnp.tril(jnp.ones((56, 56), dtype=bool))
        mask_BxS2_bk0 = jnp.logical_not(jnp.broadcast_to(_validS2[:, :], (32, 1500)))
        return (x, ctx_1024, mask_BxS2_bk0)
    x, ctx_1024, mask_BxS2_bk0 = _rec_inputs()

    def _L0_attn_setup():
        import jax, jax.numpy as jnp
        import numpy as np
        EPS = 1e-05
        N_HEADS = 16

        def _rmsnorm(x):
            return x * jax.lax.rsqrt(jnp.mean(x * x, axis=-1, keepdims=True) + 1e-06)

        def _act_quant(x):
            s = 127.0 / jnp.clip(jnp.max(jnp.abs(x), axis=-1, keepdims=True), EPS)
            xq = jnp.clip(jnp.round(x * s), -128, 127) / s
            return x + jax.lax.stop_gradient(xq - x)

        def _weight_quant(w):
            s = 1.0 / jnp.clip(jnp.mean(jnp.abs(w)), EPS)
            wq = jnp.clip(jnp.round(w * s), -1, 1) / s
            return w + jax.lax.stop_gradient(wq - w)

        def bitlinear(x, w):
            xq = _act_quant(_rmsnorm(x))
            wq = _weight_quant(w)
            return jnp.einsum('bsd,ed->bse', xq, wq)
        key = jax.random.key(seed)
        kx, kq, kk, kv, ko = jax.random.split(key, 5)
        B, S, D = (2, 512, 128)
        return {'x': jax.random.normal(kx, (B, S, D), dtype=jnp.float32), 'wq': jax.random.normal(kq, (D, D), dtype=jnp.float32) * 0.02, 'wk': jax.random.normal(kk, (D, D), dtype=jnp.float32) * 0.02, 'wv': jax.random.normal(kv, (D, D), dtype=jnp.float32) * 0.02, 'wo': jax.random.normal(ko, (D, D), dtype=jnp.float32) * 0.02}
    _L0_attn_all = _L0_attn_setup()
    _L0_attn_in = {k: v for k, v in _L0_attn_all.items() if k in ('wq', 'wk', 'wv', 'wo')}
    del _L0_attn_all

    def _L0_xattn_setup():
        import jax, jax.numpy as jnp
        import numpy as np
        B, TQ, TK, D, H = (2, 256, 256, 128, 16)
        HD = D // H
        NUM_PAD = 32
        key = jax.random.key(seed)
        ks = jax.random.split(key, 8)
        s = 0.02
        q = jax.random.normal(ks[0], (B, TQ, D), dtype=jnp.float32)
        kv = jax.random.normal(ks[1], (B, TK, D), dtype=jnp.float32)
        key_padding_mask = jnp.broadcast_to(jnp.arange(TK) >= TK - NUM_PAD, (B, TK))
        Wq = jax.random.normal(ks[2], (D, D), dtype=jnp.float32) * s
        bq = jax.random.normal(ks[3], (D,), dtype=jnp.float32) * s
        Wkv = jax.random.normal(ks[4], (D, 2 * D), dtype=jnp.float32) * s
        bkv = jax.random.normal(ks[5], (2 * D,), dtype=jnp.float32) * s
        Wo = jax.random.normal(ks[6], (D, D), dtype=jnp.float32) * s
        bo = jax.random.normal(ks[7], (D,), dtype=jnp.float32) * s
        return {'q': q, 'kv': kv, 'key_padding_mask': key_padding_mask, 'Wq': Wq, 'bq': bq, 'Wkv': Wkv, 'bkv': bkv, 'Wo': Wo, 'bo': bo}
    _L0_xattn_all = _L0_xattn_setup()
    _L0_xattn_in = {k: v for k, v in _L0_xattn_all.items() if k in ('Wq', 'bq', 'Wkv', 'bkv', 'Wo', 'bo')}
    del _L0_xattn_all

    def _L0_ffn_setup():
        import jax, jax.numpy as jnp
        import numpy as np
        TOP_K = 2

        def _moe(hidden_states, router_w, w_gate, w_up, w_down):
            B, S, D = hidden_states.shape
            E = router_w.shape[0]
            x = hidden_states.reshape(-1, D)
            T = x.shape[0]
            logits = x @ router_w.T
            probs = jax.nn.softmax(logits, axis=-1)
            top_w, top_i = jax.lax.top_k(probs, TOP_K)
            top_w = top_w / jnp.sum(top_w, axis=-1, keepdims=True)
            combine = jnp.zeros((T, E), dtype=x.dtype).at[jnp.arange(T)[:, None], top_i].add(top_w)
            out = jnp.zeros_like(x)
            for e in range(E):
                h = jax.nn.silu(x @ w_gate[e]) * (x @ w_up[e])
                out = out + combine[:, e:e + 1] * (h @ w_down[e])
            return out.reshape(B, S, D)
        key = jax.random.key(seed)
        ks = jax.random.split(key, 5)
        B, S, D, F, E = (2, 256, 128, 448, 8)
        return {'hidden_states': jax.random.normal(ks[0], (B, S, D), dtype=jnp.float32), 'router_w': jax.random.normal(ks[1], (E, D), dtype=jnp.float32) * 0.02, 'w_gate': jax.random.normal(ks[2], (E, D, F), dtype=jnp.float32) * 0.02, 'w_up': jax.random.normal(ks[3], (E, D, F), dtype=jnp.float32) * 0.02, 'w_down': jax.random.normal(ks[4], (E, F, D), dtype=jnp.float32) * 0.02}
    _L0_ffn_all = _L0_ffn_setup()
    _L0_ffn_in = {k: v for k, v in _L0_ffn_all.items() if k in ('router_w', 'w_gate', 'w_up', 'w_down')}
    del _L0_ffn_all
    return {'x': x, 'ctx_1024': ctx_1024, 'mask_BxS2_bk0': mask_BxS2_bk0, 'L0_attn_wq': _L0_attn_in['wq'], 'L0_attn_wk': _L0_attn_in['wk'], 'L0_attn_wv': _L0_attn_in['wv'], 'L0_attn_wo': _L0_attn_in['wo'], 'L0_xattn_Wq': _L0_xattn_in['Wq'], 'L0_xattn_bq': _L0_xattn_in['bq'], 'L0_xattn_Wkv': _L0_xattn_in['Wkv'], 'L0_xattn_bkv': _L0_xattn_in['bkv'], 'L0_xattn_Wo': _L0_xattn_in['Wo'], 'L0_xattn_bo': _L0_xattn_in['bo'], 'L0_ffn_router_w': _L0_ffn_in['router_w'], 'L0_ffn_w_gate': _L0_ffn_in['w_gate'], 'L0_ffn_w_up': _L0_ffn_in['w_up'], 'L0_ffn_w_down': _L0_ffn_in['w_down']}

def reference(x, ctx_1024, mask_BxS2_bk0, L0_attn_wq, L0_attn_wk, L0_attn_wv, L0_attn_wo, L0_xattn_Wq, L0_xattn_bq, L0_xattn_Wkv, L0_xattn_bkv, L0_xattn_Wo, L0_xattn_bo, L0_ffn_router_w, L0_ffn_w_gate, L0_ffn_w_up, L0_ffn_w_down):
    import jax
    import jax.numpy as jnp

    def _L0_attn_ref(x, wq, wk, wv, wo):
        import jax, jax.numpy as jnp
        import numpy as np
        EPS = 1e-05
        N_HEADS = 16

        def _rmsnorm(x):
            return x * jax.lax.rsqrt(jnp.mean(x * x, axis=-1, keepdims=True) + 1e-06)

        def _act_quant(x):
            s = 127.0 / jnp.clip(jnp.max(jnp.abs(x), axis=-1, keepdims=True), EPS)
            xq = jnp.clip(jnp.round(x * s), -128, 127) / s
            return x + jax.lax.stop_gradient(xq - x)

        def _weight_quant(w):
            s = 1.0 / jnp.clip(jnp.mean(jnp.abs(w)), EPS)
            wq = jnp.clip(jnp.round(w * s), -1, 1) / s
            return w + jax.lax.stop_gradient(wq - w)

        def bitlinear(x, w):
            xq = _act_quant(_rmsnorm(x))
            wq = _weight_quant(w)
            return jnp.einsum('bsd,ed->bse', xq, wq)
        B, S, D = x.shape
        H = N_HEADS
        Dh = D // H
        q = bitlinear(x, wq).reshape(B, S, H, Dh)
        k = bitlinear(x, wk).reshape(B, S, H, Dh)
        v = bitlinear(x, wv).reshape(B, S, H, Dh)
        scores = jnp.einsum('bshd,bstd->bsht', q, k) / Dh ** 0.5
        attn = jax.nn.softmax(scores, axis=-1)
        ctx = jnp.einsum('bsht,bstd->bshd', attn, v)
        ctx = jnp.swapaxes(ctx, 1, 2).reshape(B, S, D)
        return bitlinear(ctx, wo)

    def _L0_xattn_ref(q, kv, key_padding_mask, Wq, bq, Wkv, bkv, Wo, bo):
        import jax, jax.numpy as jnp
        import numpy as np
        B, TQ, TK, D, H = (2, 256, 256, 128, 16)
        HD = D // H
        NUM_PAD = 32
        Bc, Tq, Dm = q.shape
        Tk = kv.shape[1]
        scale = HD ** (-0.5)
        Q = (q @ Wq + bq).reshape(Bc, Tq, H, HD).transpose(0, 2, 1, 3)
        KV = (kv @ Wkv + bkv).reshape(Bc, Tk, 2, H, HD).transpose(2, 0, 3, 1, 4)
        K, V = (KV[0], KV[1])
        attn = jnp.einsum('bhqd,bhkd->bhqk', Q, K) * scale
        attn = jnp.where(key_padding_mask[:, None, None, :], -jnp.inf, attn)
        attn = jax.nn.softmax(attn, axis=-1)
        out = jnp.einsum('bhqk,bhkd->bhqd', attn, V)
        out = out.transpose(0, 2, 1, 3).reshape(Bc, Tq, Dm)
        return out @ Wo + bo

    def _L0_ffn_ref(hidden_states, router_w, w_gate, w_up, w_down):
        import jax, jax.numpy as jnp
        import numpy as np
        TOP_K = 2

        def _moe(hidden_states, router_w, w_gate, w_up, w_down):
            B, S, D = hidden_states.shape
            E = router_w.shape[0]
            x = hidden_states.reshape(-1, D)
            T = x.shape[0]
            logits = x @ router_w.T
            probs = jax.nn.softmax(logits, axis=-1)
            top_w, top_i = jax.lax.top_k(probs, TOP_K)
            top_w = top_w / jnp.sum(top_w, axis=-1, keepdims=True)
            combine = jnp.zeros((T, E), dtype=x.dtype).at[jnp.arange(T)[:, None], top_i].add(top_w)
            out = jnp.zeros_like(x)
            for e in range(E):
                h = jax.nn.silu(x @ w_gate[e]) * (x @ w_up[e])
                out = out + combine[:, e:e + 1] * (h @ w_down[e])
            return out.reshape(B, S, D)
        return _moe(hidden_states, router_w, w_gate, w_up, w_down)
    x = x + _L0_attn_ref(_layernorm(x, axis=-1), L0_attn_wq, L0_attn_wk, L0_attn_wv, L0_attn_wo)
    x = x + _L0_xattn_ref(_layernorm(x, axis=-1), ctx_1024, mask_BxS2_bk0, L0_xattn_Wq, L0_xattn_bq, L0_xattn_Wkv, L0_xattn_bkv, L0_xattn_Wo, L0_xattn_bo)
    x = x + _L0_ffn_ref(_layernorm(x, axis=-1), L0_ffn_router_w, L0_ffn_w_gate, L0_ffn_w_up, L0_ffn_w_down)
    return x

_drawn_inputs = setup_inputs


def setup_inputs(seed=0):
    import zlib

    import numpy as np

    out = dict(_drawn_inputs(seed))
    spreads = {}
    factors = {'L0_attn_wq': 8.0,
     'L0_attn_wk': 8.0,
     'L0_xattn_Wq': 8.0,
     'L0_xattn_bq': 72.1,
     'L0_xattn_bkv': 8.0,
     'L0_xattn_bo': 2.697,
     'L0_ffn_router_w': 8.0,
     'L0_ffn_w_gate': 7.345,
     'L0_ffn_w_up': 7.294,
     'L0_ffn_w_down': 7.307}
    for name, (base, spread) in spreads.items():
        noise = np.random.default_rng([zlib.crc32(name.encode()), seed]).standard_normal(out[name].shape)
        drawn = base * np.exp(spread * noise) if base else spread * noise
        out[name] = jnp.asarray(drawn.astype(out[name].dtype))
    for name, factor in factors.items():
        out[name] = (out[name] * factor).astype(out[name].dtype)
    return out
```

```python
from contextlib import ExitStack

import concourse.bass as bass
from concourse import mybir

F32 = mybir.dt.float32
BF16 = mybir.dt.bfloat16
ALU = mybir.AluOpType
ACT = mybir.ActivationFunctionType
AX = mybir.AxisListType

B, S, D = 32, 56, 128
H, HD = 16, 8
T = B * S
P = 2 * S
NT = T // P
SK = 1500
KT, KP = 12, 125
G, GT = 3, 4
GK = GT * KP
NJ = H // 2
PC = 2 * S
PR = 2 * HD
CMB = 6
K_PART = (0, 0, 0, 1, 1, 2)
Q_PART = (0, 1, 2, 0, 1, 0)
SR = CMB * PR
MASK_ROW = SR
SHIFT_ROW = SR + 1
ROWS = SR + 3
E, F = 8, 448
FT, FP = 4, 112
TC, NC = 448, 4
TPC = TC // P
SCALE = float(HD) ** -0.5
ROUND = 12582912.0
MASKED = -1.0e30


class Chain:

    def __init__(self, eng, sem):
        self.eng, self.sem, self.n, self.it, self.per = eng, sem, 0, None, 0

    def value(self):
        return self.n if self.it is None else self.n + self.it * self.per

    def mark(self, ins):
        self.n += 1
        ins.then_inc(self.sem, 1)

    def __call__(self, ins):
        self.mark(ins)
        self.eng.wait_ge(self.sem, self.value())

    def enter(self, it, per):
        self.it, self.per, self.n0 = it, per, self.n

    def leave(self, rounds):
        assert self.n - self.n0 == self.per, (self.n - self.n0, self.per)
        self.n, self.it = self.n0 + rounds * self.per, None


def decoder_kernel(nc, x, ctx, mask, wqkvo, xWq, xbq, xWk, xbk, xWv, xbv, xWo, xbo,
                   router, w_gate, w_up, w_down, ident, head_rows, expert_rank, out):
    with ExitStack() as st:
        def sb(name, shape, dt=F32):
            return st.enter_context(nc.sbuf_tensor(name, shape, dt))

        def sem(name):
            return st.enter_context(nc.semaphore(name))

        PS = st.enter_context(nc.psum_tensor("PS", [128, 8, 512], F32))

        X = sb("X", [P, NT, D])
        attnT = sb("attnT", [D, T])
        I32 = sb("I32", [128, 128])
        I16 = sb("I16", [128, 128], BF16)
        ones = sb("ones", [128, 128])
        Wq = sb("Wq", [D, D])
        Wk = sb("Wk", [D, D])
        Wv = sb("Wv", [D, D])
        Wo = sb("Wo", [D, D])
        bias = sb("bias", [128, 3])
        bo = sb("bo", [P, D])
        head_mask = sb("head_mask", [SR, 2])
        rank = sb("rank", [P, E])
        small = sb("small", [P, 14, NT])
        alpha = sb("alpha", [P, NT])
        beta = sb("beta", [P, NT])
        gamma = sb("gamma", [P, NT])
        mask_u8 = sb("mask_u8", [B, SK], mybir.dt.uint8)
        mask_b = sb("mask_b", [B, SK], BF16)
        scr_ctx = nc.dram_tensor("scr_ctx", [B, H, S, HD], F32).ap()
        scr_mask = nc.dram_tensor("scr_mask", [B, SK], BF16).ap()

        x_in, w_in, const_in, ffw_in = sem("x_in"), sem("w_in"), sem("const_in"), sem("ffw_in")
        mask_in, mask_out = sem("mask_in"), sem("mask_out")
        out_done = sem("out_done")
        dve_step, pool_step = sem("dve_step"), sem("pool_step")
        var_ready, sqrt_ready = sem("var_ready"), sem("sqrt_ready")
        wsum_in, wsum_done, wt_in, wt_mm, wt_ready = (
            sem("wsum_in"), sem("wsum_done"), sem("wt_in"), sem("wt_mm"), sem("wt_ready"))
        xq_ready, xqT_mm, xqT_ready = sem("xq_ready"), sem("xqT_mm"), sem("xqT_ready")
        qkv_mm, qkv_ready = sem("qkv_mm"), sem("qkv_ready")
        sub_ready, exp_ready, pv_ready = sem("sub_ready"), sem("exp_ready"), sem("pv_ready")
        cx_ready, cx_in = sem("cx_ready"), sem("cx_in")
        cx_out = [sem("cx_out0"), sem("cx_out1")]
        o_mm, x1_ready = sem("o_mm"), sem("x1_ready")
        xn_ready, xnT_mm, xnT_ready = sem("xn_ready"), sem("xnT_mm"), sem("xnT_ready")
        qT_mm, qT_ready, qcat_in, qcat_src = sem("qT_mm"), sem("qT_ready"), sem("qcat_in"), sem("qcat_src")
        stack_ones = sem("stack_ones")
        ctx_in = [sem("ctx_in0"), sem("ctx_in1")]
        ring_full = [sem(f"ring_full{k}") for k in range(3)]
        max_taken, mask_ready, beta_ready = sem("max_taken"), sem("mask_ready"), sem("beta_ready")
        g_mm = sem("g_mm")
        ctxT_ready, k_ready, parts_ready, v_ready = (
            sem("ctxT_ready"), sem("k_ready"), sem("parts_ready"), sem("v_ready"))
        kst_in = [sem(f"kst_in{g}") for g in range(G)]
        q_ready, max_ready, shift_ready, shift_in = (
            sem("q_ready"), sem("max_ready"), sem("shift_ready"), sem("shift_in"))
        scores_ready, probs_ready, pv_done, o_copied = (
            sem("scores_ready"), sem("probs_ready"), sem("pv_done"), sem("o_copied"))
        attn_ready, attnT_ready = sem("attn_ready"), sem("attnT_ready")
        y_mm, x2_ready = sem("y_mm"), sem("x2_ready")
        zn_ready, znT_mm, znT_ready = sem("zn_ready"), sem("znT_mm"), sem("znT_ready")
        rT_mm, rT_ready, logit_mm, logit_sub, logit_exp = (
            sem("rT_mm"), sem("rT_ready"), sem("logit_mm"), sem("logit_sub"), sem("logit_exp"))
        combine_ready = sem("combine_ready")
        ew_in = [sem("ew_in0"), sem("ew_in1")]
        gu_mm, silu_ready, h_ready, down_mm, acc_ready = (
            sem("gu_mm"), sem("silu_ready"), sem("h_ready"), sem("down_mm"), sem("acc_ready"))

        x_t = x.rearrange("b s d -> (b s) d").rearrange("(t p) d -> p t d", p=P)
        out_t = out.rearrange("b s d -> (b s) d").rearrange("(t p) d -> p t d", p=P)
        scr_rows = scr_ctx.rearrange("b h s d -> (b h s d)").rearrange("(t p c) -> p t c", p=P, c=D)

        Qcat = sb("Qcat", [SR, NJ, T], BF16)
        late = ExitStack()

        def sbl(name, shape, dt=F32):
            return late.enter_context(nc.sbuf_tensor(name, shape, dt))

        N1 = sbl("N1", [P, NT, D])
        N2 = sbl("N2", [P, NT, D])
        xq = sbl("xq", [P, NT, D], BF16)
        xqT = sbl("xqT", [D, T], BF16)
        xnT = sbl("xnT", [D, T])
        Q32 = sbl("Q32", [D, T])
        qpart = sbl("qpart", [D, 3, T], BF16)
        W4 = sbl("W4", [D, 4, D])
        W4a = sbl("W4a", [D, 4, D])
        W4q = sbl("W4q", [D, 4, D], BF16)
        W4T = sbl("W4T", [D, 4, D], BF16)
        wsum = sbl("wsum", [D, 4])
        dw = sbl("dw", [D, 4])
        iw = sbl("iw", [D, 4])
        qkv = sbl("qkv", [P, 2, 3 * D])
        prod = sbl("prod", [P, H, H, HD])
        prod2 = sbl("prod2", [P, 2, H, HD, H])
        sc = sbl("sc", [P, 2, H, H])
        pe_ = sbl("pe_", [P, 2, H, H])
        mx = sbl("mx", [P, 2, H])
        esum = sbl("esum", [P, 2, H])
        cx = sbl("cx", [P, 2, H, HD])
        rn = sbl("rn", [E, D])
        rT = sbl("rT", [D, E])
        lg = sbl("lg", [P, NT, E])
        lt = [sbl(f"lt{k}", [P, NT, E]) for k in range(6)]
        wg = sbl("wg", [D, 2, F])
        wu = sbl("wu", [D, 2, F])
        wd = sbl("wd", [FP, 2, FT, D])
        sg = sbl("sg", [FP, 2, TC])
        hT = sbl("hT", [FP, 2, FT, TC])
        tmp = sbl("tmp", [P, TPC, D])
        late.close()

        Kst = sb("Kst", [ROWS, 2, NJ, SK], BF16)
        kpart = sb("kpart", [D, 3, SK], BF16)
        K32 = sb("K32", [D, SK])
        krest = sb("krest", [D, G, GK])
        ctxT = sb("ctxT", [D, SK])
        cbuf = sb("cbuf", [KP, 2, KT, D])
        V = sb("V", [KP, 2, KT, NJ, 32])
        probs = sb("probs", [KP, 2, 2, 4 * PC])
        Qs = sb("Qs", [ROWS, 2, NJ, 2, S], BF16)
        mthird = sb("mthird", [PC, NJ, G])
        mrow = sb("mrow", [PC, NJ])
        shift = sb("shift", [NJ, 2, PC], BF16)
        osb = sb("osb", [128, 4, 64])
        rsum = sb("rsum", [S, 4, 4])
        attn = sb("attn", [P, D])

        def settled(eng, sem, value):
            eng.wait_ge(sem, value)
            eng.wait_ge(x_in, 16)

        def bank16(k):
            return PS[:, k, :].bitcast(BF16)

        CONSTS = 11
        block = st.enter_context(nc.Block())

        maxima = [("max", g, j) for g in range(G) for j in range(NJ)]
        PLAN = [["V0", "V1", "m", "m"], ["V2", "T0", "m", "m"], ["O", "T1", "m", "m"], ["A", "T2", "K0", "m", "m"],
                ["K1", "m", "m"], ["K2", "m", "m"], ["m", "m", "m"], ["m", "m", "m"], ["m", "m", "m"],
                ["m", "m", "m"], ["M"], []]
        assert sum(s.count("m") for s in PLAN) == G * NJ
        assert sum(len(s) for s in PLAN) % 3 == 0

        def wanted(kind, b):
            if kind in "TK":
                return 0 <= b + 2 < B
            if kind in "mMV":
                return 0 <= b + 1 < B
            return 0 <= b - 1 < B

        def units_of(b):
            left = list(maxima)
            slots = []
            for names in PLAN:
                units = []
                for name in names:
                    key = left.pop(0) if name == "m" else (name[0], int(name[1:] or 0))
                    if wanted(key[0] if key[0] != "max" else "m", b):
                        units.append(key)
                slots.append(units)
            return slots

        class Ring:

            def __init__(self):
                self.n, self.it, self.per = 0, None, 0

            def next(self):
                n = self.n
                self.n += 1
                return n % 3, n // 3 if self.it is None else n // 3 + self.it * (self.per // 3)

            def enter(self, it, per):
                self.it, self.per, self.n0 = it, per, self.n

            def leave(self, rounds):
                assert self.n - self.n0 == self.per and self.per % 3 == 0
                self.n, self.it = self.n0 + rounds * self.per, None

        UNITS = 2 * sum(len(s) for s in PLAN)

        def taken(kind, b):
            return {"T": lambda i: (ctxT_ready, (b + 2) * G + (i[0] + 1)),
                    "K": lambda i: (k_ready, (b + 2) * G + (i[0] + 1)),
                    "V": lambda i: (v_ready, (b + 1) * G + (i[0] + 1)),
                    "max": lambda i: (max_taken, (b + 1) * (G * NJ) + (i[0] * NJ + i[1] + 1)),
                    "M": lambda i: (shift_ready, b + 2),
                    "O": lambda i: (attn_ready, b),
                    "A": lambda i: (attnT_ready, b)}[kind]

        def walk(eng, ring, step, chain=None, per=0):
            for b in range(-2, 2):
                step(b, b)
            rounds = (B - 6) // 2
            with eng.Fori(0, rounds) as it:
                if ring:
                    ring.enter(it, UNITS)
                if chain:
                    chain.enter(it, per)
                for u in range(2):
                    step(it * 2 + (2 + u), 2 + u)
                if ring:
                    ring.leave(rounds)
                if chain:
                    chain.leave(rounds)
            for b in range(B - 4, B + 1):
                step(b, b)

        @block.sync
        def _(sp):
            sp.dma_start(X[:], x_t).then_inc(x_in, 16)
            sp.dma_start(W4[:], wqkvo.rearrange("k e d -> e k d")).then_inc(w_in, 16)
            consts = [(I32[:], ident), (Wq[:], xWq), (Wk[:], xWk), (Wv[:], xWv), (Wo[:], xWo), (bias[:, 0:1], xbq),
                      (bias[:, 1:2], xbk), (bias[:, 2:3], xbv), (bo[:], xbo.broadcast_to([P, D])),
                      (head_mask[:], head_rows), (rank[:], expert_rank.broadcast_to([P, E]))]
            assert len(consts) == CONSTS
            for dst, src in consts:
                sp.dma_start(dst, src).then_inc(const_in, 16)
            sp.dma_start(mask_u8[:], mask).then_inc(mask_in, 16)
            sp.wait_ge(mask_ready, 1)
            sp.dma_start(scr_mask, mask_b[:]).then_inc(mask_out, 16)

            with sp.Fori(0, NT // 2) as it:
                for u in range(2):
                    settled(sp, cx_ready, it * 2 + (u + 1))
                    for i in range(2):
                        dst = scr_ctx[bass.ds(it * 4 + (2 * u + i), 1)].rearrange("b h s d -> (b s) h d")
                        sp.dma_start(dst, cx[i * S:(i + 1) * S, u]).then_inc(cx_out[u], 16)
            for u in range(2):
                sp.wait_ge(cx_out[u], 16 * NT)
            sp.dma_start(N1[:], scr_rows).then_inc(cx_in, 16)

            sp.wait_ge(qcat_src, 1)
            for c in range(CMB):
                sp.dma_start(Qcat[c * PR:(c + 1) * PR, :, :], qpart[:, Q_PART[c], :]).then_inc(qcat_in, 16)
            sp.wait_ge(qcat_in, 16 * CMB)
            sp.wait_ge(mask_out, 16)
            sp.wait_ge(stack_ones, 2)

            def load_ctx(b, par):
                sp.dma_start(cbuf[:, par], ctx[bass.ds(b, 1)].rearrange("b (p k) d -> (b p) k d", k=KT)
                             ).then_inc(ctx_in[par], 16)

            def step(b, w):
                if w == -2:
                    load_ctx(0, 0)
                    load_ctx(1, 1)
                elif w + 3 < B:
                    settled(sp, ctxT_ready, (b + 2) * G)
                    load_ctx(b + 3, (w + 3) % 2)
                for g in range(G):
                    if wanted("K", w):
                        sp.wait_ge(parts_ready, (b + 2) * G + (g + 1))
                        cols = slice(g * GK, (g + 1) * GK)
                        for c in range(CMB):
                            sp.dma_start(Kst[c * PR:(c + 1) * PR, w % 2, :, cols], kpart[:, K_PART[c], cols]
                                         ).then_inc(kst_in[g], 16)
                        row = scr_mask[bass.ds(b + 2, 1), cols].unsqueeze(1).broadcast_to([1, NJ, GK])
                        sp.dma_start(Kst[MASK_ROW:MASK_ROW + 1, w % 2, :, cols], row).then_inc(kst_in[g], 16)
                    if g == 1 and wanted("M", w):
                        sp.wait_ge(shift_ready, b + 2)
                        for k in range(2):
                            sp.dma_start(Qs[SHIFT_ROW + k:SHIFT_ROW + k + 1, (w + 1) % 2].rearrange("r j i q -> r j (i q)"),
                                         shift[:, k, :]).then_inc(shift_in, 16)

            walk(sp, None, step)

            sp.wait_ge(attnT_ready, B)
            sp.dma_start(rn[:], router).then_inc(ffw_in, 16)

            def load_expert(e, par):
                sp.dma_start(wg[:, par], w_gate[bass.ds(e, 1)].rearrange("e d f -> (e d) f")).then_inc(ew_in[par], 16)
                sp.dma_start(wu[:, par], w_up[bass.ds(e, 1)].rearrange("e d f -> (e d) f")).then_inc(ew_in[par], 16)
                sp.dma_start(wd[:, par], w_down[bass.ds(e, 1)].rearrange("e (f p) d -> (e p) f d", p=FP)
                             ).then_inc(ew_in[par], 16)

            load_expert(0, 0)
            load_expert(1, 1)
            with sp.Fori(0, E // 2 - 1) as it:
                for u in range(2):
                    settled(sp, down_mm, (it * 2 + (u + 1)) * NC)
                    load_expert(it * 2 + (u + 2), u)
            sp.wait_ge(acc_ready, 2 + E * NC)
            sp.dma_start(out_t, X[:]).then_inc(out_done, 16)
            sp.wait_ge(out_done, 16)

        @block.gpsimd
        def _(pool):
            def weigh(t, u):
                pool.wait_ge(exp_ready, t + 1)
                nc.gpsimd.tensor_tensor(
                    prod2[:, u], pe_[:, u].unsqueeze(2).broadcast_to([P, H, HD, H]),
                    qkv[:, u, 2 * D:3 * D].rearrange("p (t d) -> p d t", d=HD).unsqueeze(1).broadcast_to([P, H, HD, H]),
                    ALU.mult).then_inc(pv_ready, 1)

            weigh(0, 0)
            weigh(1, 1)
            with pool.Fori(1, NT // 2) as it:
                for u in range(2):
                    pool.wait_ge(cx_ready, it * 2 + (u - 1))
                    weigh(it * 2 + u, u)

            pool.wait_ge(qcat_in, 16 * CMB)
            chain = Chain(pool, pool_step)

            def step(b, w):
                if not wanted("K", w):
                    return
                for g in range(G):
                    cols = slice(g * GK, (g + 1) * GK)
                    pool.wait_ge(k_ready, (b + 2) * G + (g + 1))
                    chain.mark(nc.gpsimd.tensor_tensor(kpart[:, 1, cols], K32[:, cols], kpart[:, 0, cols], ALU.subtract))
                    if w >= 0:
                        pool.wait_ge(scores_ready, b * KT + (g + 1) * GT)
                    chain(nc.gpsimd.tensor_tensor(krest[:, g, :], K32[:, cols], kpart[:, 0, cols], ALU.subtract))
                    nc.gpsimd.tensor_tensor(kpart[:, 2, cols], krest[:, g, :], kpart[:, 1, cols], ALU.subtract
                                            ).then_inc(parts_ready, 1)

            walk(pool, None, step, chain, 2 * 2 * G)

        @block.scalar
        def _(act):
            sqrts = [0]

            def sqrt_step():
                sqrts[0] += 1
                act.wait_ge(var_ready, sqrts[0])
                nc.scalar.activation(small[:, 1, :], small[:, 0, :], ACT.Sqrt).then_inc(sqrt_ready, 1)

            def turned(mm, done, dst, base, src16=False):
                for c in range(4):
                    act.wait_ge(mm, base + c + 1)
                    src = bank16(c)[:, 0:TC] if src16 else PS[:, c, 0:TC]
                    nc.scalar.copy(dst[:, c * TC:(c + 1) * TC], src).then_inc(done, 1)

            sqrt_step()
            sqrt_step()
            turned(xqT_mm, xqT_ready, xqT, 0, True)

            def take_qkv(t, u):
                act.wait_ge(qkv_mm, t + 1)
                nc.scalar.copy(qkv[:, u, :], PS[0:P, 4 + u, 0:3 * D]).then_inc(qkv_ready, 1)

            def exp_tile(t, u):
                act.wait_ge(sub_ready, t + 1)
                nc.scalar.activation(pe_[:, u], sc[:, u], ACT.Exp, scale=beta[:, bass.ds(t, 1)]).then_inc(exp_ready, 1)

            for t in range(2):
                take_qkv(t, t)
            act.wait_ge(beta_ready, 1)
            for t in range(2):
                exp_tile(t, t)
            with act.Fori(1, NT // 2) as it:
                for u in range(2):
                    t = it * 2 + u
                    act.wait_ge(pv_ready, it * 2 + (u - 1))
                    take_qkv(t, u)
                    act.wait_ge(cx_ready, it * 2 + (u - 1))
                    exp_tile(t, u)
            sqrt_step()
            turned(xqT_mm, xqT_ready, xqT, 4, True)
            sqrt_step()
            turned(xnT_mm, xnT_ready, xnT, 0)

            act.wait_ge(qcat_in, 16 * CMB)
            ring = Ring()

            def step(b, w):
                for kt, units in enumerate(units_of(w)):
                    if 0 <= w < B:
                        act.wait_ge(scores_ready, b * KT + (kt + 1))
                        if w > 0 or kt >= 2:
                            act.wait_ge(pv_done, b * KT + (kt - 1))
                        nc.scalar.activation(probs[:, kt % 2], PS[0:KP, 2 * (kt % 2):2 * (kt % 2) + 2, 0:4 * PC],
                                             ACT.Exp, scale=SCALE).then_inc(probs_ready, 1)
                    for kind, i in [key[:2] for key in units]:
                        k, turn = ring.next()
                        if kind not in "TKV":
                            continue
                        act.wait_ge(ring_full[k], turn + 1)
                        src = PS[:, 5 + k, 0:GK]
                        if kind == "T":
                            act_ins = nc.scalar.copy(ctxT[:, i * GK:(i + 1) * GK], src)
                            done = ctxT_ready
                        elif kind == "K":
                            if w >= -1:
                                act.wait_ge(parts_ready, (b + 1) * G + (i + 1))
                                act.wait_ge(kst_in[i], (b + 2) * 16 * (CMB + 1))
                            cols = slice(i * GK, (i + 1) * GK)
                            nc.scalar.activation(K32[:, cols], src, ACT.Identity, bias=bias[:, 1:2])
                            act_ins = nc.scalar.activation(kpart[:, 0, cols], src, ACT.Identity, bias=bias[:, 1:2])
                            done = k_ready
                        else:
                            if w >= 1:
                                act.wait_ge(pv_done, b * KT)
                            act_ins = nc.scalar.copy(
                                V[:, (w + 1) % 2, i * GT:(i + 1) * GT, :, 0:PR],
                                PS[0:KP, 5 + k, :].rearrange("p (k j c) -> p k j c", k=GT, c=PR))
                            done = v_ready
                        act_ins.then_inc(done, 1)

            walk(act, ring, step)

            sqrt_step()
            turned(znT_mm, znT_ready, xnT, 0)
            act.wait_ge(logit_sub, 1)
            nc.scalar.activation(lg[:], lt[0][:], ACT.Exp).then_inc(logit_exp, 1)
            with act.Fori(0, E // 2) as it:
                for u in range(2):
                    for k in range(NC * FT):
                        n = (it * 2 + u) * (NC * FT) + k
                        act.wait_ge(g_mm, n + 1)
                        act.wait_ge(h_ready, n + 1)
                        nc.scalar.activation(sg[:, k % 2], PS[0:FP, k % 2, 0:TC], ACT.Silu).then_inc(silu_ready, 1)

        @block.tensor
        def _(pe):
            def transposes(ready, count, mm, src, idt, done=None, n_done=0):
                pe.wait_ge(ready, count)
                for c in range(4):
                    for k in range(TPC):
                        dst = (bank16(c) if idt is I16 else PS[:, c, :])[:, k * P:(k + 1) * P]
                        last = nc.tensor.transpose(dst, src[:, c * TPC + k, :], idt[0:P, 0:P])
                    last.then_inc(mm, 1)

            pe.wait_ge(wsum_in, 1)
            nc.tensor.matmul(PS[:, 7, 0:4], ones[:], wsum[:], start=True, stop=True).then_inc(wsum_done, 1)
            pe.wait_ge(wt_in, 1)
            for k in range(4):
                last = nc.tensor.transpose(bank16(7)[:, k * D:(k + 1) * D], W4q[:, k, :], I16[:])
            last.then_inc(wt_mm, 1)
            transposes(xq_ready, 1, xqT_mm, xq, I16)
            pe.wait_ge(wt_ready, 1)
            pe.wait_ge(xqT_ready, 4)

            def qkv_tile(t, u):
                nc.tensor.matmul(PS[0:P, 4 + u, 0:3 * D], xqT[:, bass.ds(t * P, P)],
                                 W4T[:, 0:3, :].rearrange("d k e -> d (k e)"), start=True, stop=True).then_inc(qkv_mm, 1)

            for t in range(2):
                qkv_tile(t, t)
            with pe.Fori(1, NT // 2) as it:
                for u in range(2):
                    pe.wait_ge(qkv_ready, it * 2 + (u - 1))
                    qkv_tile(it * 2 + u, u)

            transposes(xq_ready, 2, xqT_mm, xq, I16)
            pe.wait_ge(xqT_ready, 8)
            for t in range(NT):
                last = nc.tensor.matmul(PS[0:P, 4 + t // 4, (t % 4) * D:(t % 4 + 1) * D], xqT[:, t * P:(t + 1) * P],
                                        W4T[:, 3, :], start=True, stop=True)
                if t % 4 == 3:
                    last.then_inc(o_mm, 1)
            transposes(xn_ready, 1, xnT_mm, N1, I32)
            for c in range(NC):
                pe.wait_ge(xnT_ready, c + 1)
                nc.tensor.matmul(PS[:, 4 + c, 0:TC], Wq[:], xnT[:, c * TC:(c + 1) * TC], start=True, stop=True
                                 ).then_inc(qT_mm, 1)

            pe.wait_ge(qcat_in, 16 * CMB)
            pe.wait_ge(stack_ones, 5)
            ring = Ring()

            def scores(b, w, kt):
                if kt == 0:
                    pe.wait_ge(shift_in, (b + 1) * 32)
                if w > 0 or kt >= 2:
                    pe.wait_ge(probs_ready, b * KT + (kt - 1))
                for j in range(NJ):
                    last = nc.tensor.matmul(PS[0:KP, 2 * (kt % 2) + j // 4, (j % 4) * PC:(j % 4 + 1) * PC],
                                            Kst[:, w % 2, j, kt * KP:(kt + 1) * KP],
                                            Qs[:, w % 2, j].rearrange("r i q -> r (i q)"), start=True, stop=True)
                last.then_inc(scores_ready, 1)

            def weigh(b, w, kt):
                if kt == 0:
                    if w > 0:
                        pe.wait_ge(o_copied, b)
                    pe.wait_ge(v_ready, (b + 1) * G)
                pe.wait_ge(probs_ready, b * KT + (kt + 1))
                pr = probs[:, kt % 2].rearrange("p a c -> p (a c)")
                for j in range(NJ):
                    r, c = j // 4, j % 4
                    last = nc.tensor.matmul(PS[32 * c:32 * c + 32, 4, r * PC:(r + 1) * PC], V[:, w % 2, kt, j, :],
                                            pr[:, j * PC:(j + 1) * PC], start=(kt == 0 and r == 0), stop=(kt == KT - 1),
                                            skip_group_check=True)
                last.then_inc(pv_done, 1)

            def unit(b, w, key):
                k, turn = ring.next()
                kind, i = key[:2]
                if len(recent) == 3:
                    old_kind, *old_i, ago = recent.pop(0)
                    pe.wait_ge(*taken(old_kind, b - ago)(old_i))
                recent.append([*key, 0])
                bk = PS[:, 5 + k, :]
                if kind == "T":
                    if i == 0:
                        pe.wait_ge(ctx_in[w % 2], ((b + 2 - w % 2) // 2 + 1) * 16 if ring.it is None
                                   else (ring.it + (w + 2) // 2 + 1) * 16)
                    for k2 in range(GT):
                        last = nc.tensor.transpose(bk[:, k2 * KP:(k2 + 1) * KP], cbuf[:, w % 2, i * GT + k2, :],
                                                   I32[0:KP, 0:KP])
                elif kind == "K":
                    pe.wait_ge(ctxT_ready, (b + 2) * G + (i + 1))
                    last = nc.tensor.matmul(bk[:, 0:GK], Wk[:], ctxT[:, i * GK:(i + 1) * GK], start=True, stop=True)
                elif kind == "V":
                    if i == 0:
                        pe.wait_ge(ctxT_ready, (b + 2) * G)
                    for k2 in range(GT):
                        kt = i * GT + k2
                        last = nc.tensor.matmul(bk[0:KP, k2 * D:(k2 + 1) * D], ctxT[:, kt * KP:(kt + 1) * KP], Wv[:],
                                                start=True, stop=True)
                elif kind == "max":
                    g, j = key[1:]
                    if g == 0 and j == 0:
                        pe.wait_ge(q_ready, b + 2)
                    if j == 0:
                        pe.wait_ge(kst_in[g], (b + 2) * 16 * (CMB + 1))
                    last = nc.tensor.matmul(bk[0:PC, 0:GK], Qs[0:MASK_ROW + 1, (w + 1) % 2, j].rearrange("r i q -> r (i q)"),
                                            Kst[0:MASK_ROW + 1, (w + 1) % 2, j, g * GK:(g + 1) * GK],
                                            start=True, stop=True)
                elif kind == "M":
                    pe.wait_ge(max_ready, b + 2)
                    last = nc.tensor.transpose(bk[0:NJ, 0:PC], mrow[:], I32[0:PC, 0:PC])
                elif kind == "O":
                    pe.wait_ge(o_copied, b)
                    for r in range(2):
                        last = nc.tensor.transpose(bk[:, r * 128:(r + 1) * 128],
                                                   osb[:, 2 * r:2 * r + 2, :].rearrange("p i q -> p (i q)"), I32[:])
                else:
                    pe.wait_ge(attn_ready, b)
                    last = nc.tensor.transpose(bk[:, 0:P], attn[:], I32[0:P, 0:P])
                last.then_inc(ring_full[k], 1)

            recent = []

            def step(b, w):
                for r in recent:
                    r[-1] += 1
                for kt, units in enumerate(units_of(w)):
                    if 0 <= w < B and kt + 1 < KT:
                        scores(b, w, kt + 1)
                    for key in units:
                        unit(b, w, key)
                    if 0 <= w < B:
                        weigh(b, w, kt)
                if wanted("M", w):
                    scores(b + 1, w + 1, 0)

            walk(pe, ring, step)

            pe.wait_ge(attnT_ready, B)
            for t in range(NT):
                last = nc.tensor.matmul(PS[0:P, t // 4, (t % 4) * D:(t % 4 + 1) * D], attnT[:, t * P:(t + 1) * P], Wo[:],
                                        start=True, stop=True)
                if t % 4 == 3:
                    last.then_inc(y_mm, 1)
            pe.wait_ge(ffw_in, 16)
            nc.tensor.transpose(PS[:, 7, 0:E], rn[:], I32[0:E, 0:E]).then_inc(rT_mm, 1)
            transposes(zn_ready, 1, znT_mm, N1, I32)
            pe.wait_ge(rT_ready, 1)
            for t in range(NT):
                if t % TPC == 0:
                    pe.wait_ge(znT_ready, t // TPC + 1)
                last = nc.tensor.matmul(PS[0:P, 6, t * E:(t + 1) * E], xnT[:, t * P:(t + 1) * P], rT[:],
                                        start=True, stop=True)
            last.then_inc(logit_mm, 1)

            with pe.Fori(0, E // 2) as it:
                for u in range(2):
                    e = it * 2 + u
                    pe.wait_ge(ew_in[u], (it + 1) * 48)

                    def down(m):
                        pe.wait_ge(h_ready, e * (NC * FT) + ((m + 1) * FT + 2))
                        pe.wait_ge(acc_ready, e * NC + (m + 1))
                        for k in range(TPC):
                            for f in range(FT):
                                last = nc.tensor.matmul(PS[0:P, 4 + m % 2, k * D:(k + 1) * D],
                                                        hT[:, m % 2, f, k * P:(k + 1) * P], wd[:, u, f, :],
                                                        start=(f == 0), stop=(f == FT - 1))
                        last.then_inc(down_mm, 1)

                    for m in range(NC):
                        for f in range(FT):
                            k = m * FT + f
                            pe.wait_ge(h_ready, e * (NC * FT) + (k + 1))
                            nc.tensor.matmul(PS[0:FP, k % 2, 0:TC], wg[:, u, f * FP:(f + 1) * FP],
                                             xnT[:, m * TC:(m + 1) * TC], start=True, stop=True).then_inc(g_mm, 1)
                            nc.tensor.matmul(PS[0:FP, 2 + k % 2, 0:TC], wu[:, u, f * FP:(f + 1) * FP],
                                             xnT[:, m * TC:(m + 1) * TC], start=True, stop=True).then_inc(gu_mm, 1)
                            if f == 1 and m > 0:
                                down(m - 1)
                    down(NC - 1)

        @block.vector
        def _(dve):
            v = nc.vector
            chain = Chain(dve, dve_step)
            sqrts = [0]

            def wide(ap):
                return ap.unsqueeze(2).broadcast_to([P, NT, D])

            def inv_sqrt(eps):
                sqrts[0] += 1
                v.tensor_scalar(small[:, 0, :], small[:, 2, :], 1.0 / D, eps, ALU.mult, ALU.add).then_inc(var_ready, 1)
                dve.wait_ge(sqrt_ready, sqrts[0])
                chain(v.reciprocal(small[:, 3, :], small[:, 1, :]))
                chain(v.tensor_tensor(small[:, 4, :], small[:, 3, :], small[:, 3, :], ALU.mult))
                chain(v.tensor_tensor(small[:, 4, :], small[:, 4, :], small[:, 0, :], ALU.mult))
                chain(v.tensor_scalar(small[:, 4, :], small[:, 4, :], -0.5, 1.5, ALU.mult, ALU.add))
                chain(v.tensor_tensor(small[:, 3, :], small[:, 3, :], small[:, 4, :], ALU.mult))

            def layernorm(src, done=None):
                chain(v.tensor_reduce(small[:, 2, :], src[:], AX.X, ALU.add))
                chain(v.tensor_scalar(small[:, 2, :], small[:, 2, :], 1.0 / D, None, ALU.mult))
                chain(v.tensor_tensor(N1[:], src[:], wide(small[:, 2, :]), ALU.subtract))
                chain(v.tensor_tensor(N2[:], N1[:], N1[:], ALU.mult))
                chain(v.tensor_reduce(small[:, 2, :], N2[:], AX.X, ALU.add))
                inv_sqrt(1e-5)
                ins = v.tensor_tensor(N1[:], N1[:], wide(small[:, 3, :]), ALU.mult)
                if done is None:
                    chain(ins)
                else:
                    ins.then_inc(done, 1)

            def quantise(step_size):
                chain(v.tensor_tensor(N2[:], N1[:], N1[:], ALU.mult))
                chain(v.tensor_reduce(small[:, 2, :], N2[:], AX.X, ALU.add))
                inv_sqrt(1e-6)
                chain(v.tensor_tensor(N1[:], N1[:], wide(small[:, 3, :]), ALU.mult))
                chain(v.scalar_tensor_tensor(out=N2[:], in0=N1[:], scalar=-1.0, in1=N1[:], op0=ALU.mult, op1=ALU.max))
                chain(v.tensor_reduce(small[:, 5, :], N2[:], AX.X, ALU.max))
                chain(v.tensor_scalar(small[:, 5, :], small[:, 5, :], 1e-5, None, ALU.max))
                chain(v.reciprocal(small[:, 6, :], small[:, 5, :]))
                chain(v.tensor_scalar(small[:, 6, :], small[:, 6, :], 127.0, None, ALU.mult))
                chain(v.tensor_scalar(step_size[:], small[:, 5, :], 1.0 / 127.0, None, ALU.mult))
                chain(v.tensor_tensor(N1[:], N1[:], wide(small[:, 6, :]), ALU.mult))
                chain(v.tensor_scalar(N2[:], N1[:], ROUND, ROUND, ALU.add, ALU.subtract))
                v.tensor_scalar(xq[:], N2[:], 127.0, -128.0, ALU.min, ALU.max).then_inc(xq_ready, 1)

            chain(v.memset(ones[:], 1.0))
            dve.wait_ge(w_in, 16)
            chain(v.scalar_tensor_tensor(out=W4a[:], in0=W4[:], scalar=-1.0, in1=W4[:], op0=ALU.mult, op1=ALU.max))
            v.tensor_reduce(wsum[:], W4a[:], AX.X, ALU.add).then_inc(wsum_in, 1)
            dve.wait_ge(const_in, 16 * CONSTS)
            chain(v.tensor_copy(I16[:], I32[:]))
            dve.wait_ge(wsum_done, 1)
            chain(v.tensor_scalar(dw[:], PS[:, 7, 0:4], 1.0 / (D * D), 1e-5, ALU.mult, ALU.max))
            chain(v.reciprocal(iw[:], dw[:]))
            for k in range(4):
                chain(v.tensor_scalar(W4[:, k, :], W4[:, k, :], iw[:, k:k + 1], ROUND, ALU.mult, ALU.add))
            chain(v.tensor_scalar(W4[:], W4[:], ROUND, 1.0, ALU.subtract, ALU.min))
            v.tensor_scalar(W4q[:], W4[:], -1.0, None, ALU.max).then_inc(wt_in, 1)

            dve.wait_ge(mask_in, 16)
            v.tensor_scalar(mask_b[:].rearrange("b (k p) -> b p k", p=KP),
                            mask_u8[:].rearrange("b (p k) -> b p k", k=KT), MASKED, None, ALU.mult).then_inc(mask_ready, 1)

            dve.wait_ge(wt_mm, 1)
            v.tensor_copy(W4T[:].rearrange("d k e -> d (k e)"), bank16(7)[:, 0:4 * D]).then_inc(wt_ready, 1)

            dve.wait_ge(x_in, 16)
            layernorm(X)
            quantise(alpha)
            chain(v.tensor_scalar(gamma[:], alpha[:], dw[0:P, 2:3], None, ALU.mult))
            chain(v.tensor_tensor(beta[:], alpha[:], alpha[:], ALU.mult))
            chain(v.tensor_scalar(beta[:], beta[:], dw[0:P, 0:1], dw[0:P, 1:2], ALU.mult, ALU.mult))
            v.tensor_scalar(beta[:], beta[:], SCALE, None, ALU.mult).then_inc(beta_ready, 1)

            def head_scores(t, u):
                dve.wait_ge(qkv_ready, t + 1)
                q = qkv[:, u, 0:D].rearrange("p (h d) -> p h d", d=HD).unsqueeze(2).broadcast_to([P, H, H, HD])
                k = qkv[:, u, D:2 * D].rearrange("p (h d) -> p h d", d=HD).unsqueeze(1).broadcast_to([P, H, H, HD])
                chain(v.tensor_tensor(prod[:], q, k, ALU.mult))
                chain(v.tensor_reduce(sc[:, u], prod[:], AX.X, ALU.add))
                chain(v.tensor_reduce(mx[:, u], sc[:, u], AX.X, ALU.max))
                v.tensor_tensor(sc[:, u], sc[:, u], mx[:, u].unsqueeze(2).broadcast_to([P, H, H]), ALU.subtract
                                ).then_inc(sub_ready, 1)

            def head_output(t, u, stored):
                dve.wait_ge(pv_ready, t + 1)
                chain(v.tensor_reduce(esum[:, u], pe_[:, u], AX.X, ALU.add))
                chain(v.reciprocal(esum[:, u], esum[:, u]))
                if stored is not None:
                    dve.wait_ge(cx_out[u], stored)
                chain(v.tensor_reduce(cx[:, u], prod2[:, u], AX.X, ALU.add))
                v.scalar_tensor_tensor(out=cx[:, u], in0=cx[:, u], scalar=gamma[:, bass.ds(t, 1)],
                                       in1=esum[:, u].unsqueeze(2).broadcast_to([P, H, HD]), op0=ALU.mult, op1=ALU.mult
                                       ).then_inc(cx_ready, 1)

            head_scores(0, 0)
            head_scores(1, 1)
            head_output(0, 0, None)
            with dve.Fori(1, NT // 2) as it:
                chain.enter(it - 1, 12)
                for u in range(2):
                    head_scores(it * 2 + u, u)
                    head_output(it * 2 + (u - 1), 1 - u, (it - 1 + u) * 32)
                chain.leave(NT // 2 - 1)
            head_output(NT - 1, 1, 32 * (NT // 2 - 1))

            dve.wait_ge(cx_in, 16)
            quantise(alpha)
            chain(v.tensor_scalar(gamma[:], alpha[:], dw[0:P, 3:4], None, ALU.mult))
            for t in range(NT):
                if t % 4 == 0:
                    dve.wait_ge(o_mm, t // 4 + 1)
                ins = v.scalar_tensor_tensor(out=X[:, t, :], in0=PS[0:P, 4 + t // 4, (t % 4) * D:(t % 4 + 1) * D],
                                             scalar=gamma[:, t:t + 1], in1=X[:, t, :], op0=ALU.mult, op1=ALU.add)
            chain(ins)

            layernorm(X, xn_ready)
            for c in range(NC):
                dve.wait_ge(qT_mm, c + 1)
                cols = slice(c * TC, (c + 1) * TC)
                chain(v.tensor_scalar(Q32[:, cols], PS[:, 4 + c, 0:TC], bias[:, 0:1], None, ALU.add))
            chain(v.tensor_copy(qpart[:, 0, :], Q32[:]))
            chain(v.tensor_tensor(Q32[:], Q32[:], qpart[:, 0, :], ALU.subtract))
            chain(v.tensor_copy(qpart[:, 1, :], Q32[:]))
            v.tensor_tensor(qpart[:, 2, :], Q32[:], qpart[:, 1, :], ALU.subtract).then_inc(qcat_src, 1)
            dve.wait_ge(qcat_in, 16 * CMB)
            v.memset(Kst[SR:ROWS], 1.0).then_inc(stack_ones, 1)
            v.memset(Qs[SR:ROWS], 1.0).then_inc(stack_ones, 1)
            v.memset(V[:], 1.0).then_inc(stack_ones, 1)
            v.memset(osb[:], 0.0).then_inc(stack_ones, 1)
            v.memset(attn[:], 0.0).then_inc(stack_ones, 1)
            dve.wait_ge(stack_ones, 5)

            ring = Ring()

            def step(b, w):
                if wanted("M", w):
                    if w >= 1:
                        dve.wait_ge(scores_ready, b * KT)
                    for i in range(2):
                        q = Qcat[:, :, bass.ds((b + 1) * S, S)]
                        ins = v.tensor_scalar(Qs[0:SR, (w + 1) % 2, :, i, :], q, head_mask[:, i:i + 1], None, ALU.mult)
                        if i == 0:
                            chain.mark(ins)
                        else:
                            ins.then_inc(q_ready, 1)
                if w >= 1:
                    dve.wait_ge(pv_done, b * KT)
                    v.tensor_copy(osb[:, :, 0:S], PS[:, 4, 0:2 * PC].rearrange("p (a q) -> p a q", q=S)).then_inc(o_copied, 1)
                for units in units_of(w):
                    for key in units:
                        k, turn = ring.next()
                        kind = key[0]
                        if kind in "TKV":
                            continue
                        dve.wait_ge(ring_full[k], turn + 1)
                        bk = PS[:, 5 + k, :]
                        if kind == "max":
                            g, j = key[1:]
                            ins = v.tensor_reduce(mthird[:, j, g:g + 1], bk[0:PC, 0:GK], AX.X, ALU.max)
                            ins.then_inc(max_taken, 1)
                            if g == G - 1 and j == NJ - 1:
                                dve.wait_ge(max_taken, (b + 2) * (G * NJ))
                                v.tensor_reduce(mrow[:], mthird[:], AX.X, ALU.max).then_inc(max_ready, 1)
                        elif kind == "M":
                            if w >= 0:
                                dve.wait_ge(shift_in, (b + 1) * 32)
                            chain(v.tensor_scalar(shift[:, 0, :], bk[0:NJ, 0:PC], -1.0, None, ALU.mult))
                            v.scalar_tensor_tensor(out=shift[:, 1, :], in0=bk[0:NJ, 0:PC], scalar=-1.0,
                                                   in1=shift[:, 0, :], op0=ALU.mult, op1=ALU.subtract
                                                   ).then_inc(shift_ready, 1)
                        elif kind == "O":
                            to = attn[0:S, :].rearrange("q (r c i d) -> q r c i d", r=2, c=4, i=2)
                            for i in range(2):
                                pv = bk[64 * i:64 * i + S, 0:256].rearrange("q (r c e) -> q r c e", r=2, e=32)
                                chain(v.reciprocal(rsum[:, 2 * i:2 * i + 2, :], pv[:, :, :, PR]))
                                ins = v.tensor_tensor(to[:, :, :, i, :], pv[:, :, :, i * HD:(i + 1) * HD],
                                                      rsum[:, 2 * i:2 * i + 2, :].unsqueeze(3).broadcast_to([S, 2, 4, HD]),
                                                      ALU.mult)
                                if i == 0:
                                    chain.mark(ins)
                                else:
                                    ins.then_inc(attn_ready, 1)
                        else:
                            v.tensor_scalar(attnT[:, bass.ds((b - 1) * S, S)], bk[:, 0:S], bias[:, 2:3], None, ALU.add
                                            ).then_inc(attnT_ready, 1)

            walk(dve, ring, step, chain, 10)

            for t in range(NT):
                if t % 4 == 0:
                    dve.wait_ge(y_mm, t // 4 + 1)
                ins = v.tensor_tensor(X[:, t, :], PS[0:P, t // 4, (t % 4) * D:(t % 4 + 1) * D], X[:, t, :], ALU.add)
            chain(ins)
            chain(v.tensor_tensor(X[:], X[:], bo[:].unsqueeze(1).broadcast_to([P, NT, D]), ALU.add))
            layernorm(X, zn_ready)
            dve.wait_ge(rT_mm, 1)
            v.tensor_copy(rT[:], PS[:, 7, 0:E]).then_inc(rT_ready, 1)

            def per_token(k):
                return small[:, k, :].unsqueeze(2).broadcast_to([P, NT, E])

            dve.wait_ge(logit_mm, 1)
            logits = PS[0:P, 6, 0:NT * E].rearrange("p (t e) -> p t e", e=E)
            chain(v.tensor_reduce(small[:, 7, :], logits, AX.X, ALU.max))
            v.tensor_tensor(lt[0][:], logits, per_token(7), ALU.subtract).then_inc(logit_sub, 1)
            dve.wait_ge(logit_exp, 1)
            chain(v.tensor_reduce(small[:, 8, :], lg[:], AX.X, ALU.add))
            chain(v.reciprocal(small[:, 8, :], small[:, 8, :]))
            chain(v.tensor_tensor(lg[:], lg[:], per_token(8), ALU.mult))
            ranks = rank[:].unsqueeze(1).broadcast_to([P, NT, E])
            for best in range(2):
                src, hit, sel = lg if best == 0 else lt[3], lt[1], lt[2 + 2 * best]
                chain(v.tensor_reduce(small[:, 9 + best, :], src[:], AX.X, ALU.max))
                chain(v.tensor_tensor(hit[:], src[:], per_token(9 + best), ALU.is_equal))
                chain(v.tensor_tensor(hit[:], hit[:], ranks, ALU.mult))
                chain(v.tensor_reduce(small[:, 11, :], hit[:], AX.X, ALU.max))
                chain(v.tensor_tensor(sel[:], ranks, per_token(11), ALU.is_equal))
                if best == 0:
                    chain(v.scalar_tensor_tensor(out=lt[3][:], in0=sel[:], scalar=-2.0, in1=lg[:],
                                                 op0=ALU.mult, op1=ALU.add))
                chain(v.tensor_tensor(sel[:], sel[:], per_token(9 + best), ALU.mult))
            chain(v.tensor_tensor(small[:, 12, :], small[:, 9, :], small[:, 10, :], ALU.add))
            chain(v.reciprocal(small[:, 12, :], small[:, 12, :]))
            chain(v.tensor_tensor(lt[5][:], lt[2][:], lt[4][:], ALU.add))
            chain(v.tensor_tensor(lt[5][:], lt[5][:], per_token(12), ALU.mult))
            v.memset(hT[:], 0.0).then_inc(h_ready, 2)
            v.memset(tmp[:], 0.0).then_inc(acc_ready, 2)
            dve.wait_ge(h_ready, 2)
            dve.wait_ge(acc_ready, 2)
            with dve.Fori(0, E // 2) as it:
                chain.enter(it, 2 * NC)
                for u in range(2):
                    e = it * 2 + u

                    def accumulate(m):
                        dve.wait_ge(down_mm, e * NC + (m + 1))
                        weight = lt[5][:, m * TPC:(m + 1) * TPC, bass.ds(e, 1)].broadcast_to([P, TPC, D])
                        chain(v.tensor_tensor(tmp[:], PS[0:P, 4 + m % 2, :].rearrange("p (t d) -> p t d", d=D),
                                              weight, ALU.mult))
                        rows = X[:, m * TPC:(m + 1) * TPC, :]
                        v.tensor_tensor(rows, rows, tmp[:], ALU.add).then_inc(acc_ready, 1)

                    for m in range(NC):
                        for f in range(FT):
                            k = m * FT + f
                            dve.wait_ge(silu_ready, e * (NC * FT) + (k + 1))
                            dve.wait_ge(gu_mm, e * (NC * FT) + (k + 1))
                            v.tensor_tensor(hT[:, m % 2, f, :], sg[:, k % 2], PS[0:FP, 2 + k % 2, 0:TC], ALU.mult
                                            ).then_inc(h_ready, 1)
                            if f == 2 and m > 0:
                                accumulate(m - 1)
                    accumulate(NC - 1)
                chain.leave(E // 2)


def kernel(x, ctx_1024, mask_BxS2_bk0, L0_attn_wq, L0_attn_wk, L0_attn_wv, L0_attn_wo, L0_xattn_Wq, L0_xattn_bq,
           L0_xattn_Wkv, L0_xattn_bkv, L0_xattn_Wo, L0_xattn_bo, L0_ffn_router_w, L0_ffn_w_gate, L0_ffn_w_up,
           L0_ffn_w_down):
    import numpy as np
    import concourse.bacc as bacc
    from concourse.bass_utils import run_bass_kernel_spmd

    def by_row(w):
        return w.reshape(w.shape[0], NJ, PR).transpose(0, 2, 1).reshape(w.shape[0], D)

    f = np.asarray
    kv = f(L0_xattn_Wkv)
    bkv = f(L0_xattn_bkv)
    arrays = {
        "x": f(x), "ctx": f(ctx_1024), "mask": f(mask_BxS2_bk0),
        "wqkvo": np.stack([f(L0_attn_wq), f(L0_attn_wk), f(L0_attn_wv), f(L0_attn_wo)]),
        "xWq": by_row(f(L0_xattn_Wq)), "xbq": by_row(f(L0_xattn_bq)[None]).T,
        "xWk": by_row(kv[:, :D]), "xbk": by_row(bkv[None, :D]).T,
        "xWv": kv[:, D:], "xbv": bkv[D:, None],
        "xWo": f(L0_xattn_Wo), "xbo": f(L0_xattn_bo)[None],
        "router": f(L0_ffn_router_w), "w_gate": f(L0_ffn_w_gate), "w_up": f(L0_ffn_w_up), "w_down": f(L0_ffn_w_down),
        "ident": np.eye(128, dtype=np.float32),
        "head_rows": ((np.arange(SR)[:, None] // HD) % 2 == np.arange(2)[None]).astype(np.float32),
        "expert_rank": np.arange(E, 0, -1).astype(np.float32)[None],
    }
    arrays = {k: np.ascontiguousarray(v) for k, v in arrays.items()}
    nc = bacc.Bacc("TRN2", target_bir_lowering=False, num_devices=1)
    args = {k: nc.dram_tensor(k, v.shape, mybir.dt.from_np(v.dtype), kind="ExternalInput").ap()
            for k, v in arrays.items()}
    out = nc.dram_tensor("out", (B, S, D), F32, kind="ExternalOutput").ap()
    decoder_kernel(nc, out=out, **args)
    r = run_bass_kernel_spmd(nc, [arrays], core_ids=[0])
    return r.results[0]["out"]
```

```python
from contextlib import ExitStack

import concourse.bass as bass
from concourse import mybir

F32 = mybir.dt.float32
BF16 = mybir.dt.bfloat16
ALU = mybir.AluOpType
ACT = mybir.ActivationFunctionType
AX = mybir.AxisListType

B, S, D = 32, 56, 128
H, HD = 16, 8
T = B * S
P = 2 * S
NT = T // P
SK = 1500
KT, KP = 12, 125
G, GT = 3, 4
GK = GT * KP
NJ = H // 2
PC = 2 * S
PR = 2 * HD
CMB = 6
K_PART = (0, 0, 0, 1, 1, 2)
Q_PART = (0, 1, 2, 0, 1, 0)
SR = CMB * PR
MASK_ROW = SR
SHIFT_ROW = SR + 1
ROWS = SR + 3
E, F = 8, 448
FT, FP = 4, 112
TC, NC = 448, 4
TPC = TC // P
SCALE = float(HD) ** -0.5
ROUND = 12582912.0
MASKED = -1.0e30


class Chain:

    def __init__(self, eng, sem):
        self.eng, self.sem, self.n, self.it, self.per = eng, sem, 0, None, 0

    def value(self):
        return self.n if self.it is None else self.n + self.it * self.per

    def mark(self, ins):
        self.n += 1
        ins.then_inc(self.sem, 1)

    def __call__(self, ins):
        self.mark(ins)
        self.eng.wait_ge(self.sem, self.value())

    def enter(self, it, per):
        self.it, self.per, self.n0 = it, per, self.n

    def leave(self, rounds):
        assert self.n - self.n0 == self.per, (self.n - self.n0, self.per)
        self.n, self.it = self.n0 + rounds * self.per, None


def decoder_kernel(nc, x, ctx, mask, wqkvo, xWq, xbq, xWk, xbk, xWv, xbv, xWo, xbo,
                   router, w_gate, w_up, w_down, ident, head_rows, expert_rank, out):
    with ExitStack() as st:
        def sb(name, shape, dt=F32):
            return st.enter_context(nc.sbuf_tensor(name, shape, dt))

        def sem(name):
            return st.enter_context(nc.semaphore(name))

        PS = st.enter_context(nc.psum_tensor("PS", [128, 8, 512], F32))

        X = sb("X", [P, NT, D])
        attnT = sb("attnT", [D, T])
        I32 = sb("I32", [128, 128])
        I16 = sb("I16", [128, 128], BF16)
        ones = sb("ones", [128, 128])
        Wq = sb("Wq", [D, D])
        Wk = sb("Wk", [D, D])
        Wv = sb("Wv", [D, D])
        Wo = sb("Wo", [D, D])
        bias = sb("bias", [128, 3])
        bo = sb("bo", [P, D])
        head_mask = sb("head_mask", [SR, 2])
        rank = sb("rank", [P, E])
        small = sb("small", [P, 14, NT])
        alpha = sb("alpha", [P, NT])
        beta = sb("beta", [P, NT])
        gamma = sb("gamma", [P, NT])
        mask_b = sb("mask_b", [B, SK], BF16)
        scr_ctx = nc.dram_tensor("scr_ctx", [B, H, S, HD], F32).ap()
        scr_mask = nc.dram_tensor("scr_mask", [B, SK], BF16).ap()

        x_in, w_in, const_in, ffw_in = sem("x_in"), sem("w_in"), sem("const_in"), sem("ffw_in")
        mask_in, mask_out = sem("mask_in"), sem("mask_out")
        out_done = sem("out_done")
        dve_step, pool_step = sem("dve_step"), sem("pool_step")
        var_ready, sqrt_ready = sem("var_ready"), sem("sqrt_ready")
        wsum_in, wsum_done, wt_in, wt_mm, wt_ready = (
            sem("wsum_in"), sem("wsum_done"), sem("wt_in"), sem("wt_mm"), sem("wt_ready"))
        xq_ready, xqT_ready = sem("xq_ready"), sem("xqT_ready")
        qkv_ready = sem("qkv_ready")
        sub_ready, exp_ready, pv_ready = sem("sub_ready"), sem("exp_ready"), sem("pv_ready")
        mul_ready, q32_ready = sem("mul_ready"), sem("q32_ready")
        cx_ready, cx_in = sem("cx_ready"), sem("cx_in")
        cx_out = [sem("cx_out0"), sem("cx_out1")]
        x1_ready, xn_ready, xnT_ready = sem("x1_ready"), sem("xn_ready"), sem("xnT_ready")
        qcat_in, qcat_src = sem("qcat_in"), sem("qcat_src")
        stack_ones = sem("stack_ones")
        ctx_in = [sem("ctx_in0"), sem("ctx_in1")]
        ring_full = [sem(f"ring_full{k}") for k in range(3)]
        max_taken, mask_ready = sem("max_taken"), sem("mask_ready")
        g_mm = sem("g_mm")
        ctxT_ready, k_ready, parts_ready, v_ready = (
            sem("ctxT_ready"), sem("k_ready"), sem("parts_ready"), sem("v_ready"))
        kst_in = [sem(f"kst_in{g}") for g in range(G)]
        q_ready, max_ready, shift_ready, shift_in = (
            sem("q_ready"), sem("max_ready"), sem("shift_ready"), sem("shift_in"))
        scores_ready, probs_ready, pv_done, o_copied = (
            sem("scores_ready"), sem("probs_ready"), sem("pv_done"), sem("o_copied"))
        attn_ready, attnT_ready = sem("attn_ready"), sem("attnT_ready")
        x2_ready = sem("x2_ready")
        zn_ready, znT_mm, znT_ready = sem("zn_ready"), sem("znT_mm"), sem("znT_ready")
        rT_mm, rT_ready, logit_mm, logit_sub, logit_exp = (
            sem("rT_mm"), sem("rT_ready"), sem("logit_mm"), sem("logit_sub"), sem("logit_exp"))
        ew_in = [sem("ew_in0"), sem("ew_in1")]
        gu_mm, silu_ready, h_ready, down_mm, acc_ready = (
            sem("gu_mm"), sem("silu_ready"), sem("h_ready"), sem("down_mm"), sem("acc_ready"))

        x_t = x.rearrange("b s d -> (b s) d").rearrange("(t p) d -> p t d", p=P)
        out_t = out.rearrange("b s d -> (b s) d").rearrange("(t p) d -> p t d", p=P)
        scr_rows = scr_ctx.rearrange("b h s d -> (b h s d)").rearrange("(t p c) -> p t c", p=P, c=D)

        xq = sb("xq", [P, NT, D], BF16)
        W4T = sb("W4T", [D, 4, D], BF16)
        wsum = sb("wsum", [D, 4])
        dw = sb("dw", [D, 4])
        iw = sb("iw", [D, 4])
        g1 = sb("g1", [P, TPC, D])
        g2 = sb("g2", [P, TPC, D])
        xqg = sb("xqg", [P, TPC, D], BF16)
        xqT = sb("xqT", [D, TC], BF16)
        xnTg = sb("xnTg", [D, TC])
        Q32 = sb("Q32", [D, TC])
        qpart = sb("qpart", [D, 3, TC], BF16)
        Qcat = sb("Qcat", [SR, NJ, TC], BF16)
        qkv = sb("qkv", [P, 2, 3 * D])
        weights = ExitStack()

        def sbw(name, shape, dt=F32):
            return weights.enter_context(nc.sbuf_tensor(name, shape, dt))

        W4 = sbw("W4", [D, 4, D])
        W4a = sbw("W4a", [D, 4, D])
        W4q = sbw("W4q", [D, 4, D], BF16)
        mask_u8 = sbw("mask_u8", [B, SK], mybir.dt.uint8)
        weights.close()
        prod = sb("prod", [P, H, H, HD])
        prod2 = sb("prod2", [P, H, HD, H])
        sc = sb("sc", [P, H, H])
        pe_ = sb("pe_", [P, H, H])
        mx = sb("mx", [P, H])
        esum = sb("esum", [P, H])
        cx = sb("cx", [P, 2, H, HD])

        early = ExitStack()

        def sbe(name, shape, dt=F32):
            return early.enter_context(nc.sbuf_tensor(name, shape, dt))

        N1 = sbe("N1", [P, NT, D])
        early.close()
        V = sb("V", [KP, 2, KT, NJ, 32])

        late = ExitStack()

        def sbl(name, shape, dt=F32):
            return late.enter_context(nc.sbuf_tensor(name, shape, dt))

        xnT = sbl("xnT", [D, T])
        rn = sbl("rn", [E, D])
        rT = sbl("rT", [D, E])
        lg = sbl("lg", [P, NT, E])
        lt = [sbl(f"lt{k}", [P, NT, E]) for k in range(6)]
        wg = sbl("wg", [D, 2, F])
        wu = sbl("wu", [D, 2, F])
        wd = sbl("wd", [FP, 2, FT, D])
        sg = sbl("sg", [FP, 2, TC])
        hT = sbl("hT", [FP, 2, FT, TC])
        tmp = sbl("tmp", [P, TPC, D])
        late.close()

        Kst = sb("Kst", [ROWS, 2, NJ, SK], BF16)
        kpart = sb("kpart", [D, 3, SK], BF16)
        K32 = sb("K32", [D, SK])
        krest = sb("krest", [D, 2, GK])
        ctxT = sb("ctxT", [D, SK])
        cbuf = sb("cbuf", [KP, 2, KT, D])
        probs = sb("probs", [KP, 2, 2, 4 * PC])
        Qs = sb("Qs", [ROWS, 2, NJ, 2, S], BF16)
        mthird = sb("mthird", [PC, NJ, G])
        mrow = sb("mrow", [PC, NJ])
        shift = sb("shift", [NJ, 2, PC], BF16)
        osb = sb("osb", [128, 4, 64])
        rsum = sb("rsum", [S, 4, 4])
        attn = sb("attn", [P, D])

        def multiply_heads(api, eng, t, u, half):
            eng.wait_ge(qkv_ready, t + 1)
            hh = H // 2
            q = qkv[:, u, half * hh * HD:(half + 1) * hh * HD].rearrange("p (h d) -> p h d", d=HD)
            k = qkv[:, u, D:2 * D].rearrange("p (h d) -> p h d", d=HD)
            return api.tensor_tensor(prod[:, half * hh:(half + 1) * hh], q.unsqueeze(2).broadcast_to([P, hh, H, HD]),
                                     k.unsqueeze(1).broadcast_to([P, hh, H, HD]), ALU.mult)

        def weigh_heads(api, eng, t, u):
            eng.wait_ge(exp_ready, t + 1)
            return api.tensor_tensor(
                prod2[:], pe_[:].unsqueeze(2).broadcast_to([P, H, HD, H]),
                qkv[:, u, 2 * D:3 * D].rearrange("p (t d) -> p d t", d=HD).unsqueeze(1).broadcast_to([P, H, HD, H]),
                ALU.mult)

        def settled(eng, sem, value):
            eng.wait_ge(sem, value)
            eng.wait_ge(x_in, 16)

        def bank16(k):
            return PS[:, k, :].bitcast(BF16)

        CONSTS = 11
        DVE_STEPS = 8 * 5 + TPC * 8 + 31
        block = st.enter_context(nc.Block())

        RINGED = ("T", "K", "V", "m", "M", "O", "A", "gX", "gq", "gY", "gW", "gN", "gQ", "Y")
        maxima = [(g, j) for g in range(G) for j in range(NJ)]
        BASE = [
            "C Z V0 V1 V2 T0 E m m B m m m",
            "T1 m O",
            "T2 m K0",
            "m m m K1 m",
            "m K2 m S0",
            "m S1 m m",
            "A m m",
            "m m m P0",
            "m m",
            "m",
            "S2 M R",
            "P1 P2"]
        GROUP = {
            1: {0: "gc", 1: "gX gq_0", 3: "w1_0 gs0_0 gs1_0", 4: "gs2_0", 5: "gs3_0", 6: "gx_0 w2_0", 9: "gq_1",
                10: "go0_0", 11: "go1_0"},
            2: {0: "w1_1", 2: "gs0_1", 3: "gs1_1 gs2_1", 4: "gs3_1", 5: "st_0 gx_1", 8: "w2_1", 10: "go0_1",
                11: "gq_2 go1_1"},
            3: {0: "w1_2", 1: "st_1", 2: "gs0_2", 3: "gs1_2", 4: "gs2_2 gs3_2", 5: "gx_2", 6: "w2_2 gq_3",
                7: "w1_3", 10: "go0_2 go1_2 st_2"},
            4: {1: "gs0_3", 3: "gs1_3 gs2_3", 4: "gs3_3", 7: "gx_3 w2_3", 10: "go0_3 go1_3 st_3 ld"},
            5: {2: "qa0 gr", 3: "qa1 qa2", 4: "qa3 qa4", 6: "gY gW", 9: "ln0", 10: "ln1", 11: "gr ln2"},
            6: {1: "gN", 3: "gQ sp0", 4: "sp1", 7: "qc"},
            7: {},
            8: {}}
        FIRST = {
            -2: ["C ga0_0 gr ga1_0 gr ga2_0 ga3_0 ga4_0 ga5_0 gc gX gq_0 gq_1 w1_0 gs0_0 gs1_0 gs2_0 gs3_0 T0 "
                 "gx_0 w2_0 ga0_1 gr ga1_1 T1 go0_0 go1_0 st_0 w1_1 gs0_1 gr ga2_1 gs1_1 gs2_1 ga3_1 ga4_1 ga5_1 "
                 "gs3_1 K0 T2 gx_1 w2_1 ga0_2 gr ga1_2 gr gq_2 ga2_2 K1 K2 S0 S1 go0_1 go1_1 P0 w1_2 gs0_2 ga3_2 "
                 "gs1_2 P1 gs2_2 gs3_2 ga4_2 ga5_2 gx_2 gq_3 st_1 w1_3 gs0_3 gs1_3 gs2_3 gs3_3 w2_2 gx_3 go0_2 "
                 "w2_3 go1_2 S2 ga0_3 gr go0_3 st_2 ga1_3 gr ga2_3 P2 ga3_3 ga4_3 ga5_3 go1_3 st_3 ld"],
            -1: ["C V0 V1 V2 T0 T1 K0 qa0 S0 gr qa1 qa2 T2 K1 P0 qa3 K2 qa4 S1 gY gW ln0 ln1 gr P1 ln2 gN gQ "
                 "sp0 sp1 qc Z m m m m m m m m m m S2 m m m m m m m m m P2 m m m m m M R"],
        }

        LAST = {B - 1: {3 * c + 2: f"Y{c}" for c in range(NC - 1)}, B: {KT - 1: f"Y{NC - 1}"}}

        def wanted(kind, b):
            if kind in ("T", "K", "S", "P"):
                return 0 <= b + 2 < B
            if kind == "C":
                return b + 3 < B
            if kind in ("m", "M", "R", "V", "Z"):
                return 0 <= b + 1 < B
            if kind in ("O", "A", "E"):
                return 0 <= b - 1 < B
            if kind == "B":
                return 0 <= b < B
            return True

        def plan(w, grouped):
            added = GROUP[w] if grouped else LAST.get(w, {})
            texts = FIRST.get(w) or [t + " " + added.get(k, "") for k, t in enumerate(BASE)]
            left, slots = list(maxima), []
            for text in texts:
                items = []
                for name in text.split():
                    if name == "m":
                        kind, numbers = "m", left.pop(0)
                    else:
                        kind = name.rstrip("0123456789_")
                        if name[:2] in ("w1", "w2"):
                            kind, numbers = name[:2], (int(name[3:]),)
                        else:
                            numbers = tuple(int(x) for x in name[len(kind):].split("_") if x)
                    if wanted(kind, w):
                        items.append((kind, numbers))
                slots.append(items)
            return slots

        class Ring:

            def __init__(self):
                self.n, self.it, self.per = 0, None, 0

            def next(self):
                n = self.n
                self.n += 1
                return n % 3, n // 3 if self.it is None else n // 3 + self.it * (self.per // 3)

            def enter(self, it, per):
                self.it, self.per, self.n0 = it, per, self.n

            def leave(self, rounds):
                assert self.n - self.n0 == self.per and self.per % 3 == 0, self.n - self.n0
                self.n, self.it = self.n0 + rounds * self.per, None

        START_ROOTS = 2 * (B // 8) + 2

        class Roots:

            def __init__(self):
                self.n = 0

            def next(self, w, gi):
                self.n += 1
                return self.n if w < 1 else (gi - 1) * 2 + self.n

        LOOP = 8
        ROUNDS = B // LOOP - 1
        UNITS = sum(kind in RINGED for w in range(1, 1 + LOOP) for slot in plan(w, True) for kind, _ in slot)

        assert len({tuple([item for slot in plan(w, w > 0) for item in slot if item[0] in RINGED][-3:])
                    for w in (0, LOOP)}) == 1

        def taken(kind, b, gi, i):
            return {"T": lambda: (ctxT_ready, (b + 2) * G + (i[0] + 1)),
                    "K": lambda: (k_ready, (b + 2) * G + (i[0] + 1)),
                    "V": lambda: (v_ready, (b + 1) * G + (i[0] + 1)),
                    "m": lambda: (max_taken, (b + 1) * (G * NJ) + (i[0] * NJ + i[1] + 1)),
                    "M": lambda: (shift_ready, b + 2),
                    "O": lambda: (attn_ready, b),
                    "A": lambda: (attnT_ready, b),
                    "gX": lambda: (xqT_ready, gi * 2 + 1),
                    "gY": lambda: (xqT_ready, gi * 2 + 2),
                    "gq": lambda: (qkv_ready, gi * TPC + (i[0] + 1)),
                    "gW": lambda: (x1_ready, gi + 1),
                    "gN": lambda: (xnT_ready, gi + 1),
                    "gQ": lambda: (q32_ready, gi + 1),
                    "Y": lambda: (x2_ready, i[0] + 1)}[kind]()

        def walk(eng, ring, step, chain=None, per=0):
            for w in range(-2, 1):
                step(w, w, 0, plan(w, False))
            with eng.Fori(0, ROUNDS) as it:
                if ring:
                    ring.enter(it, UNITS)
                if chain:
                    chain.enter(it, per)
                for w in range(1, 1 + LOOP):
                    step(it * LOOP + w, w, it + 1, plan(w, True))
                if ring:
                    ring.leave(ROUNDS)
                if chain:
                    chain.leave(ROUNDS)
            for w in range(1 + LOOP * ROUNDS, B + 1):
                step(w, w, B // LOOP, plan(w, False))

        @block.sync
        def _(sp):
            sp.dma_start(X[:], x_t).then_inc(x_in, 16)
            sp.dma_start(W4[:], wqkvo.rearrange("k e d -> e k d")).then_inc(w_in, 16)
            consts = [(I32[:], ident), (Wq[:], xWq), (Wk[:], xWk), (Wv[:], xWv), (Wo[:], xWo), (bias[:, 0:1], xbq),
                      (bias[:, 1:2], xbk), (bias[:, 2:3], xbv), (bo[:], xbo.broadcast_to([P, D])),
                      (head_mask[:], head_rows), (rank[:], expert_rank.broadcast_to([P, E]))]
            assert len(consts) == CONSTS
            for dst, src in consts:
                sp.dma_start(dst, src).then_inc(const_in, 16)
            sp.dma_start(mask_u8[:], mask).then_inc(mask_in, 16)
            sp.wait_ge(mask_ready, 1)
            sp.dma_start(scr_mask, mask_b[:]).then_inc(mask_out, 16)

            sp.wait_ge(mask_out, 16)

            def load_ctx(b, par):
                sp.dma_start(cbuf[:, par], ctx[bass.ds(b, 1)].rearrange("b (p k) d -> (b p) k d", k=KT)
                             ).then_inc(ctx_in[par], 16)

            def step(b, w, gi, slots):
                for kind, i in [item for slot in slots for item in slot]:
                    if kind == "C":
                        if w == -2:
                            load_ctx(0, 0)
                            load_ctx(1, 1)
                        else:
                            settled(sp, ctxT_ready, (b + 2) * G)
                            load_ctx(b + 3, (w + 3) % 2)
                    elif kind == "P":
                        g = i[0]
                        if w == -2 and g == 0:
                            sp.wait_ge(stack_ones, 1)
                        sp.wait_ge(parts_ready, (b + 2) * G + (g + 1))
                        cols = slice(g * GK, (g + 1) * GK)
                        for c in range(CMB):
                            sp.dma_start(Kst[c * PR:(c + 1) * PR, w % 2, :, cols], kpart[:, K_PART[c], cols]
                                         ).then_inc(kst_in[g], 16)
                        row = scr_mask[bass.ds(b + 2, 1), cols].unsqueeze(1).broadcast_to([1, NJ, GK])
                        sp.dma_start(Kst[MASK_ROW:MASK_ROW + 1, w % 2, :, cols], row).then_inc(kst_in[g], 16)
                    elif kind == "R":
                        sp.wait_ge(shift_ready, b + 2)
                        for k in range(2):
                            sp.dma_start(Qs[SHIFT_ROW + k:SHIFT_ROW + k + 1, (w + 1) % 2].rearrange("r j i q -> r j (i q)"),
                                         shift[:, k, :]).then_inc(shift_in, 16)
                    elif kind == "st":
                        u = i[0] % 2
                        settled(sp, cx_ready, gi * TPC + (i[0] + 1))
                        for half in range(2):
                            dst = scr_ctx[bass.ds(gi * (2 * TPC) + (2 * i[0] + half), 1)].rearrange("b h s d -> (b s) h d")
                            sp.dma_start(dst, cx[half * S:(half + 1) * S, u]).then_inc(cx_out[u], 16)
                    elif kind == "ld":
                        settled(sp, cx_out[0], (gi + 1) * (TPC * 16))
                        settled(sp, cx_out[1], (gi + 1) * (TPC * 16))
                        sp.dma_start(g1[:], scr_rows[:, bass.ds(gi * TPC, TPC), :]).then_inc(cx_in, 16)
                    elif kind == "qc":
                        sp.wait_ge(qcat_src, gi + 1)
                        for c in range(CMB):
                            sp.dma_start(Qcat[c * PR:(c + 1) * PR, :, :], qpart[:, Q_PART[c], :]).then_inc(qcat_in, 16)

            walk(sp, None, step)

            sp.wait_ge(attnT_ready, B)
            sp.dma_start(rn[:], router).then_inc(ffw_in, 16)

            def load_expert(e, par):
                sp.dma_start(wg[:, par], w_gate[bass.ds(e, 1)].rearrange("e d f -> (e d) f")).then_inc(ew_in[par], 16)
                sp.dma_start(wu[:, par], w_up[bass.ds(e, 1)].rearrange("e d f -> (e d) f")).then_inc(ew_in[par], 16)
                sp.dma_start(wd[:, par], w_down[bass.ds(e, 1)].rearrange("e (f p) d -> (e p) f d", p=FP)
                             ).then_inc(ew_in[par], 16)

            load_expert(0, 0)
            load_expert(1, 1)
            with sp.Fori(0, E // 2 - 1) as it:
                for u in range(2):
                    settled(sp, down_mm, (it * 2 + (u + 1)) * NC)
                    load_expert(it * 2 + (u + 2), u)
            for m in range(NC):
                sp.wait_ge(acc_ready, 2 + (E - 1) * NC + (m + 1))
                tiles = slice(m * TPC, (m + 1) * TPC)
                sp.dma_start(out_t[:, tiles, :], X[:, tiles, :]).then_inc(out_done, 16)
            sp.wait_ge(out_done, 16 * NC)

        @block.gpsimd
        def _(pool):
            chain = Chain(pool, pool_step)
            for dst, value in ((Kst[SR:ROWS], 1.0), (Qs[SR:ROWS], 1.0), (osb[:], 0.0), (V[:], 1.0)):
                chain(nc.gpsimd.memset(dst, value))
            nc.gpsimd.memset(attn[:], 0.0).then_inc(stack_ones, 1)

            def step(b, w, gi, slots):
                for kind, i in [item for slot in slots for item in slot]:
                    t = gi * TPC + i[0] if i else None
                    if kind == "S":
                        g = i[0]
                        cols = slice(g * GK, (g + 1) * GK)
                        pool.wait_ge(k_ready, (b + 2) * G + (g + 1))
                        chain.mark(nc.gpsimd.tensor_tensor(kpart[:, 1, cols], K32[:, cols], kpart[:, 0, cols],
                                                           ALU.subtract))
                        if w >= 0:
                            pool.wait_ge(scores_ready, b * KT + (g + 1) * GT)
                        chain(nc.gpsimd.tensor_tensor(krest[:, (w + g) % 2, :], K32[:, cols], kpart[:, 0, cols], ALU.subtract))
                        nc.gpsimd.tensor_tensor(kpart[:, 2, cols], krest[:, (w + g) % 2, :], kpart[:, 1, cols], ALU.subtract
                                                ).then_inc(parts_ready, 1)
                    elif kind == "w1":
                        if not (w < 0 and i[0] == 0):
                            pool.wait_ge(sub_ready, t)
                        multiply_heads(nc.gpsimd, pool, t, i[0] % 2, 1).then_inc(mul_ready, 1)
                    elif kind == "w2":
                        if not (w < 0 and i[0] == 0):
                            pool.wait_ge(cx_ready, t)
                        weigh_heads(nc.gpsimd, pool, t, i[0] % 2).then_inc(pv_ready, 1)

            walk(pool, None, step, chain, LOOP * 2 * G)

        @block.scalar
        def _(act):
            ring = Ring()

            def exponentials(b, w, kt):
                act.wait_ge(scores_ready, b * KT + (kt + 1))
                if w > 0 or kt >= 2:
                    act.wait_ge(pv_done, b * KT + (kt - 1))
                nc.scalar.activation(probs[:, kt % 2], PS[0:KP, 2 * (kt % 2):2 * (kt % 2) + 2, 0:4 * PC],
                                     ACT.Exp, scale=SCALE).then_inc(probs_ready, 1)

            def step(b, w, gi, slots):
                for kt, items in enumerate(slots):
                    if 0 <= w < B and kt > 0:
                        exponentials(b, w, kt)
                    for kind, i in items:
                        if kind in RINGED:
                            k, turn = ring.next()
                            src = PS[:, 5 + k, 0:GK]
                        t = gi * TPC + i[0] if i else None
                        if kind in ("T", "K", "V", "gX", "gY", "gq", "gN"):
                            act.wait_ge(ring_full[k], turn + 1)
                        if kind == "B":
                            exponentials(b, w, 0)
                        elif kind == "T":
                            nc.scalar.copy(ctxT[:, i[0] * GK:(i[0] + 1) * GK], src).then_inc(ctxT_ready, 1)
                        elif kind == "K":
                            g = i[0]
                            if w >= -1:
                                act.wait_ge(parts_ready, (b + 1) * G + (g + 1))
                                act.wait_ge(kst_in[g], (b + 2) * 16 * (CMB + 1))
                            cols = slice(g * GK, (g + 1) * GK)
                            nc.scalar.activation(K32[:, cols], src, ACT.Identity, bias=bias[:, 1:2])
                            nc.scalar.activation(kpart[:, 0, cols], src, ACT.Identity, bias=bias[:, 1:2]
                                                 ).then_inc(k_ready, 1)
                        elif kind == "V":
                            if w == -1 and i[0] == 0:
                                act.wait_ge(stack_ones, 1)
                            if w >= 1:
                                act.wait_ge(pv_done, b * KT)
                            nc.scalar.copy(V[:, (w + 1) % 2, i[0] * GT:(i[0] + 1) * GT, :, 0:PR],
                                           PS[0:KP, 5 + k, :].rearrange("p (k j c) -> p k j c", k=GT, c=PR)
                                           ).then_inc(v_ready, 1)
                        elif kind in ("gX", "gY"):
                            nc.scalar.copy(xqT[:], bank16(5 + k)[:, 0:TC]).then_inc(xqT_ready, 1)
                        elif kind == "gN":
                            nc.scalar.copy(xnTg[:], PS[:, 5 + k, 0:TC]).then_inc(xnT_ready, 1)
                        elif kind == "gq":
                            if w > 0 or i[0] >= 2:
                                act.wait_ge(cx_ready, t - 1)
                            nc.scalar.copy(qkv[:, i[0] % 2, :], PS[0:P, 5 + k, 0:3 * D]).then_inc(qkv_ready, 1)
                        elif kind == "gx":
                            act.wait_ge(sub_ready, t + 1)
                            if not (w < 0 and i[0] == 0):
                                act.wait_ge(cx_ready, t)
                            nc.scalar.activation(pe_[:], sc[:], ACT.Exp, scale=beta[:, bass.ds(t, 1)]
                                                 ).then_inc(exp_ready, 1)
                        elif kind == "gr":
                            act.wait_ge(var_ready, roots.next(w, gi))
                            nc.scalar.activation(small[:, 1, 0:TPC], small[:, 0, 0:TPC], ACT.Sqrt).then_inc(sqrt_ready, 1)

            roots = Roots()
            walk(act, ring, step)

            def turned(mm, done, dst):
                for c in range(4):
                    act.wait_ge(mm, c + 1)
                    nc.scalar.copy(dst[:, c * TC:(c + 1) * TC], PS[:, c, 0:TC]).then_inc(done, 1)

            act.wait_ge(var_ready, START_ROOTS + 2 * ROUNDS + 1)
            nc.scalar.activation(small[:, 1, :], small[:, 0, :], ACT.Sqrt).then_inc(sqrt_ready, 1)
            turned(znT_mm, znT_ready, xnT)
            act.wait_ge(logit_sub, 1)
            nc.scalar.activation(lg[:], lt[0][:], ACT.Exp).then_inc(logit_exp, 1)
            with act.Fori(0, E // 2) as it:
                for u in range(2):
                    for k in range(NC * FT):
                        n = (it * 2 + u) * (NC * FT) + k
                        act.wait_ge(g_mm, n + 1)
                        act.wait_ge(h_ready, n + 1)
                        nc.scalar.activation(sg[:, k % 2], PS[0:FP, k % 2, 0:TC], ACT.Silu).then_inc(silu_ready, 1)

        @block.tensor
        def _(pe):
            pe.wait_ge(wsum_in, 1)
            nc.tensor.matmul(PS[:, 7, 0:4], ones[:], wsum[:], start=True, stop=True).then_inc(wsum_done, 1)
            pe.wait_ge(wt_in, 1)
            for k in range(4):
                last = nc.tensor.transpose(bank16(7)[:, k * D:(k + 1) * D], W4q[:, k, :], I16[:])
            last.then_inc(wt_mm, 1)
            pe.wait_ge(wt_ready, 1)
            ring = Ring()

            def scores(b, w, kt):
                if kt == 0:
                    pe.wait_ge(shift_in, (b + 1) * 32)
                if w > 0 or kt >= 2:
                    pe.wait_ge(probs_ready, b * KT + (kt - 1))
                for j in range(NJ):
                    last = nc.tensor.matmul(PS[0:KP, 2 * (kt % 2) + j // 4, (j % 4) * PC:(j % 4 + 1) * PC],
                                            Kst[:, w % 2, j, kt * KP:(kt + 1) * KP],
                                            Qs[:, w % 2, j].rearrange("r i q -> r (i q)"), start=True, stop=True)
                last.then_inc(scores_ready, 1)

            def weigh(b, w, kt):
                if kt == 0:
                    if w > 0:
                        pe.wait_ge(o_copied, b)
                    pe.wait_ge(v_ready, (b + 1) * G)
                pe.wait_ge(probs_ready, b * KT + (kt + 1))
                pr = probs[:, kt % 2].rearrange("p a c -> p (a c)")
                for j in range(NJ):
                    r, c = j // 4, j % 4
                    last = nc.tensor.matmul(PS[32 * c:32 * c + 32, 4, r * PC:(r + 1) * PC], V[:, w % 2, kt, j, :],
                                            pr[:, j * PC:(j + 1) * PC], start=(kt == 0 and r == 0), stop=(kt == KT - 1),
                                            skip_group_check=True)
                last.then_inc(pv_done, 1)

            def unit(b, w, gi, kind, i):
                k, turn = ring.next()
                if len(recent) == 3:
                    old_kind, old_i, old_gi, ago = recent.pop(0)
                    pe.wait_ge(*taken(old_kind, b - ago, old_gi, old_i))
                recent.append([kind, i, gi, 0])
                bk = PS[:, 5 + k, :]
                if kind == "T":
                    if i[0] == 0:
                        pe.wait_ge(ctx_in[w % 2], ((w + 2) // 2 + 1) * 16 if ring.it is None
                                   else ring.it * (LOOP // 2 * 16) + ((w + 2) // 2 + 1) * 16)
                    for k2 in range(GT):
                        last = nc.tensor.transpose(bk[:, k2 * KP:(k2 + 1) * KP], cbuf[:, w % 2, i[0] * GT + k2, :],
                                                   I32[0:KP, 0:KP])
                elif kind == "K":
                    g = i[0]
                    pe.wait_ge(ctxT_ready, (b + 2) * G + (g + 1))
                    last = nc.tensor.matmul(bk[:, 0:GK], Wk[:], ctxT[:, g * GK:(g + 1) * GK], start=True, stop=True)
                elif kind == "V":
                    if i[0] == 0:
                        pe.wait_ge(ctxT_ready, (b + 2) * G)
                    for k2 in range(GT):
                        kt = i[0] * GT + k2
                        last = nc.tensor.matmul(bk[0:KP, k2 * D:(k2 + 1) * D], ctxT[:, kt * KP:(kt + 1) * KP], Wv[:],
                                                start=True, stop=True)
                elif kind == "m":
                    g, j = i
                    if g == 0 and j == 0:
                        if w == -1:
                            pe.wait_ge(stack_ones, 1)
                        pe.wait_ge(q_ready, b + 2)
                    if j == 0:
                        pe.wait_ge(kst_in[g], (b + 2) * 16 * (CMB + 1))
                    last = nc.tensor.matmul(bk[0:PC, 0:GK], Qs[0:MASK_ROW + 1, (w + 1) % 2, j].rearrange("r i q -> r (i q)"),
                                            Kst[0:MASK_ROW + 1, (w + 1) % 2, j, g * GK:(g + 1) * GK],
                                            start=True, stop=True)
                elif kind == "M":
                    pe.wait_ge(max_ready, b + 2)
                    last = nc.tensor.transpose(bk[0:NJ, 0:PC], mrow[:], I32[0:PC, 0:PC])
                elif kind == "O":
                    pe.wait_ge(o_copied, b)
                    for r in range(2):
                        last = nc.tensor.transpose(bk[:, r * 128:(r + 1) * 128],
                                                   osb[:, 2 * r:2 * r + 2, :].rearrange("p i q -> p (i q)"), I32[:])
                elif kind == "A":
                    pe.wait_ge(attn_ready, b)
                    last = nc.tensor.transpose(bk[:, 0:P], attn[:], I32[0:P, 0:P])
                elif kind in ("gX", "gY"):
                    pe.wait_ge(xq_ready, gi * 2 + (1 if kind == "gX" else 2))
                    for k2 in range(TPC):
                        last = nc.tensor.transpose(bank16(5 + k)[:, k2 * P:(k2 + 1) * P], xqg[:, k2, :], I16[0:P, 0:P])
                elif kind == "gq":
                    if i[0] == 0:
                        pe.wait_ge(xqT_ready, gi * 2 + 1)
                    last = nc.tensor.matmul(bk[0:P, 0:3 * D], xqT[:, i[0] * P:(i[0] + 1) * P],
                                            W4T[:, 0:3, :].rearrange("d k e -> d (k e)"), start=True, stop=True)
                elif kind == "gW":
                    pe.wait_ge(xqT_ready, gi * 2 + 2)
                    for k2 in range(TPC):
                        last = nc.tensor.matmul(bk[0:P, k2 * D:(k2 + 1) * D], xqT[:, k2 * P:(k2 + 1) * P], W4T[:, 3, :],
                                                start=True, stop=True)
                elif kind == "gN":
                    pe.wait_ge(xn_ready, gi + 1)
                    for k2 in range(TPC):
                        last = nc.tensor.transpose(bk[:, k2 * P:(k2 + 1) * P], g1[:, k2, :], I32[0:P, 0:P])
                elif kind == "Y":
                    pe.wait_ge(attnT_ready, (i[0] + 1) * (2 * TPC))
                    for k2 in range(TPC):
                        t = i[0] * TPC + k2
                        last = nc.tensor.matmul(bk[0:P, k2 * D:(k2 + 1) * D], attnT[:, t * P:(t + 1) * P], Wo[:],
                                                start=True, stop=True)
                else:
                    pe.wait_ge(xnT_ready, gi + 1)
                    last = nc.tensor.matmul(bk[:, 0:TC], Wq[:], xnTg[:], start=True, stop=True)
                last.then_inc(ring_full[k], 1)

            recent = []

            def step(b, w, gi, slots):
                for r in recent:
                    r[-1] += 1
                for kt, items in enumerate(slots):
                    if 0 <= w < B and 0 < kt < KT - 1:
                        scores(b, w, kt + 1)
                    for kind, i in items:
                        if kind == "B":
                            scores(b, w, 0)
                            scores(b, w, 1)
                        elif kind in RINGED:
                            unit(b, w, gi, kind, i)
                    if 0 <= w < B:
                        weigh(b, w, kt)

            walk(pe, ring, step)

            pe.wait_ge(probs_ready, B * KT)
            pe.wait_ge(x2_ready, NC)
            pe.wait_ge(ffw_in, 16)
            nc.tensor.transpose(PS[:, 7, 0:E], rn[:], I32[0:E, 0:E]).then_inc(rT_mm, 1)
            for c in range(NC):
                pe.wait_ge(zn_ready, c + 1)
                for k in range(TPC):
                    last = nc.tensor.transpose(PS[:, c, k * P:(k + 1) * P], N1[:, c * TPC + k, :], I32[0:P, 0:P])
                last.then_inc(znT_mm, 1)
            pe.wait_ge(rT_ready, 1)
            for t in range(NT):
                if t % TPC == 0:
                    pe.wait_ge(znT_ready, t // TPC + 1)
                last = nc.tensor.matmul(PS[0:P, 6, t * E:(t + 1) * E], xnT[:, t * P:(t + 1) * P], rT[:],
                                        start=True, stop=True)
            last.then_inc(logit_mm, 1)

            with pe.Fori(0, E // 2) as it:
                for u in range(2):
                    e = it * 2 + u
                    pe.wait_ge(ew_in[u], (it + 1) * 48)

                    def down(m):
                        pe.wait_ge(h_ready, e * (NC * FT) + ((m + 1) * FT + 2))
                        pe.wait_ge(acc_ready, e * NC + (m + 1))
                        for k in range(TPC):
                            for f in range(FT):
                                last = nc.tensor.matmul(PS[0:P, 4 + m % 2, k * D:(k + 1) * D],
                                                        hT[:, m % 2, f, k * P:(k + 1) * P], wd[:, u, f, :],
                                                        start=(f == 0), stop=(f == FT - 1))
                        last.then_inc(down_mm, 1)

                    for m in range(NC):
                        for f in range(FT):
                            k = m * FT + f
                            pe.wait_ge(h_ready, e * (NC * FT) + (k + 1))
                            nc.tensor.matmul(PS[0:FP, k % 2, 0:TC], wg[:, u, f * FP:(f + 1) * FP],
                                             xnT[:, m * TC:(m + 1) * TC], start=True, stop=True).then_inc(g_mm, 1)
                            nc.tensor.matmul(PS[0:FP, 2 + k % 2, 0:TC], wu[:, u, f * FP:(f + 1) * FP],
                                             xnT[:, m * TC:(m + 1) * TC], start=True, stop=True).then_inc(gu_mm, 1)
                            if f == 1 and m > 0:
                                down(m - 1)
                    down(NC - 1)

        @block.vector
        def _(dve):
            v = nc.vector
            chain = Chain(dve, dve_step)

            def inv_sqrt(n, count):
                dve.wait_ge(sqrt_ready, count)
                chain(v.reciprocal(small[:, 3, :n], small[:, 1, :n]))
                chain(v.tensor_tensor(small[:, 4, :n], small[:, 3, :n], small[:, 3, :n], ALU.mult))
                chain(v.tensor_tensor(small[:, 4, :n], small[:, 4, :n], small[:, 0, :n], ALU.mult))
                chain(v.tensor_scalar(small[:, 4, :n], small[:, 4, :n], -0.5, 1.5, ALU.mult, ALU.add))
                chain(v.tensor_tensor(small[:, 3, :n], small[:, 3, :n], small[:, 4, :n], ALU.mult))

            def spread(k, n):
                return small[:, k, :n].unsqueeze(2).broadcast_to([P, n, D])

            def centre(src, dst, n):
                chain(v.tensor_reduce(small[:, 2, :n], src, AX.X, ALU.add))
                chain(v.tensor_scalar(small[:, 2, :n], small[:, 2, :n], 1.0 / D, None, ALU.mult))
                chain(v.tensor_tensor(dst, src, spread(2, n), ALU.subtract))

            def variance(src, square, n, eps):
                chain(v.tensor_tensor(square, src, src, ALU.mult))
                chain(v.tensor_reduce(small[:, 2, :n], square, AX.X, ALU.add))
                v.tensor_scalar(small[:, 0, :n], small[:, 2, :n], 1.0 / D, eps, ALU.mult, ALU.add).then_inc(var_ready, 1)

            def largest(src, size, n):
                chain(v.scalar_tensor_tensor(out=size, in0=src, scalar=-1.0, in1=src, op0=ALU.mult, op1=ALU.max))
                chain(v.tensor_reduce(small[:, 5, :n], size, AX.X, ALU.max))
                chain(v.tensor_scalar(small[:, 5, :n], small[:, 5, :n], 1e-5, None, ALU.max))
                chain(v.reciprocal(small[:, 6, :n], small[:, 5, :n]))
                chain(v.tensor_scalar(small[:, 6, :n], small[:, 6, :n], 127.0, None, ALU.mult))

            def rounded(src, whole, n):
                chain(v.tensor_tensor(src, src, spread(6, n), ALU.mult))
                chain(v.tensor_scalar(whole, src, ROUND, ROUND, ALU.add, ALU.subtract))

            chain(v.memset(ones[:], 1.0))
            dve.wait_ge(w_in, 16)
            chain(v.scalar_tensor_tensor(out=W4a[:], in0=W4[:], scalar=-1.0, in1=W4[:], op0=ALU.mult, op1=ALU.max))
            v.tensor_reduce(wsum[:], W4a[:], AX.X, ALU.add).then_inc(wsum_in, 1)
            dve.wait_ge(const_in, 16 * CONSTS)
            chain(v.tensor_copy(I16[:], I32[:]))
            dve.wait_ge(wsum_done, 1)
            chain(v.tensor_scalar(dw[:], PS[:, 7, 0:4], 1.0 / (D * D), 1e-5, ALU.mult, ALU.max))
            chain(v.reciprocal(iw[:], dw[:]))
            for k in range(4):
                chain(v.tensor_scalar(W4[:, k, :], W4[:, k, :], iw[:, k:k + 1], ROUND, ALU.mult, ALU.add))
            chain(v.tensor_scalar(W4[:], W4[:], ROUND, 1.0, ALU.subtract, ALU.min))
            v.tensor_scalar(W4q[:], W4[:], -1.0, None, ALU.max).then_inc(wt_in, 1)

            dve.wait_ge(mask_in, 16)
            v.tensor_scalar(mask_b[:].rearrange("b (k p) -> b p k", p=KP),
                            mask_u8[:].rearrange("b (p k) -> b p k", k=KT), MASKED, None, ALU.mult).then_inc(mask_ready, 1)

            dve.wait_ge(wt_mm, 1)
            v.tensor_copy(W4T[:].rearrange("d k e -> d (k e)"), bank16(7)[:, 0:4 * D]).then_inc(wt_ready, 1)

            dve.wait_ge(x_in, 16)

            roots = Roots()

            def group_item(kind, i, w, gi, k, turn):
                t = gi * TPC + i[-1] if i else None
                rows = X[:, bass.ds(gi * TPC, TPC), :] if kind == "gW" else None
                own = slice(i[1] * TPC, (i[1] + 1) * TPC) if kind == "ga" else None
                hh = H // 2
                if kind == "ga" and i[0] == 0:
                    centre(X[:, own, :], g1[:], TPC)
                    variance(g1[:], g2[:], TPC, 1e-5)
                elif kind == "ga" and i[0] in (1, 2):
                    inv_sqrt(TPC, roots.next(w, gi))
                    chain(v.tensor_tensor(g1[:], g1[:], spread(3, TPC), ALU.mult))
                    if i[0] == 1:
                        variance(g1[:], g2[:], TPC, 1e-6)
                elif kind == "ga" and i[0] == 3:
                    largest(g1[:], g2[:], TPC)
                    chain(v.tensor_scalar(alpha[:, own], small[:, 5, :TPC], 1.0 / 127.0, None, ALU.mult))
                elif kind == "ga" and i[0] == 4:
                    rounded(g1[:], g2[:], TPC)
                    chain(v.tensor_scalar(xq[:, own, :], g2[:], 127.0, -128.0, ALU.min, ALU.max))
                elif kind == "ga":
                    chain(v.tensor_scalar(gamma[:, own], alpha[:, own], dw[0:P, 2:3], None, ALU.mult))
                    chain(v.tensor_tensor(beta[:, own], alpha[:, own], alpha[:, own], ALU.mult))
                    chain(v.tensor_scalar(beta[:, own], beta[:, own], dw[0:P, 0:1], dw[0:P, 1:2], ALU.mult, ALU.mult))
                    chain(v.tensor_scalar(beta[:, own], beta[:, own], SCALE, None, ALU.mult))
                elif kind == "gc":
                    v.tensor_copy(xqg[:], xq[:, bass.ds(gi * TPC, TPC), :]).then_inc(xq_ready, 1)
                elif kind == "gs" and i[0] == 0:
                    chain(multiply_heads(v, dve, t, i[1] % 2, 0))
                elif kind == "gs" and i[0] < 3:
                    half = i[0] - 1
                    if half == 0 and not (w < 0 and i[1] == 0):
                        dve.wait_ge(exp_ready, t)
                    if half == 1:
                        dve.wait_ge(mul_ready, t + 1)
                    chain(v.tensor_reduce(sc[:, half * hh:(half + 1) * hh], prod[:, half * hh:(half + 1) * hh], AX.X, ALU.add))
                elif kind == "gs":
                    chain(v.tensor_reduce(mx[:], sc[:], AX.X, ALU.max))
                    v.tensor_tensor(sc[:], sc[:], mx[:].unsqueeze(2).broadcast_to([P, H, H]), ALU.subtract
                                    ).then_inc(sub_ready, 1)
                elif kind == "go" and i[0] == 0:
                    dve.wait_ge(pv_ready, t + 1)
                    chain(v.tensor_reduce(esum[:], pe_[:], AX.X, ALU.add))
                    chain(v.reciprocal(esum[:], esum[:]))
                    u = i[1] % 2
                    if w > 0 or i[1] >= 2:
                        dve.wait_ge(cx_out[u], gi * (TPC * 16) + (i[1] // 2) * 32)
                    chain(v.tensor_reduce(cx[:, u, 0:hh], prod2[:, 0:hh], AX.X, ALU.add))
                elif kind == "go":
                    u = i[1] % 2
                    chain(v.tensor_reduce(cx[:, u, hh:H], prod2[:, hh:H], AX.X, ALU.add))
                    v.scalar_tensor_tensor(out=cx[:, u], in0=cx[:, u], scalar=gamma[:, bass.ds(t, 1)],
                                           in1=esum[:].unsqueeze(2).broadcast_to([P, H, HD]), op0=ALU.mult, op1=ALU.mult
                                           ).then_inc(cx_ready, 1)
                elif kind == "qa" and i[0] == 0:
                    dve.wait_ge(cx_in, (gi + 1) * 16)
                    variance(g1[:], g2[:], TPC, 1e-6)
                elif kind == "qa" and i[0] == 1:
                    inv_sqrt(TPC, roots.next(w, gi))
                    chain(v.tensor_tensor(g1[:], g1[:], spread(3, TPC), ALU.mult))
                elif kind == "qa" and i[0] == 2:
                    largest(g1[:], g2[:], TPC)
                    chain(v.tensor_scalar(small[:, 7, :TPC], small[:, 5, :TPC], 1.0 / 127.0, dw[0:P, 3:4], ALU.mult, ALU.mult))
                elif kind == "qa" and i[0] == 3:
                    rounded(g1[:], g2[:], TPC)
                elif kind == "qa":
                    v.tensor_scalar(xqg[:], g2[:], 127.0, -128.0, ALU.min, ALU.max).then_inc(xq_ready, 1)
                elif kind == "gW":
                    dve.wait_ge(ring_full[k], turn + 1)
                    chain(v.tensor_tensor(g2[:], PS[0:P, 5 + k, :].rearrange("p (t d) -> p t d", d=D), spread(7, TPC),
                                          ALU.mult))
                    chain.mark(v.tensor_tensor(g1[:], rows, g2[:], ALU.add))
                    dve.wait_ge(dve_step, chain.value())
                    v.tensor_tensor(rows, g1[:], bo[:].unsqueeze(1).broadcast_to([P, TPC, D]), ALU.add
                                    ).then_inc(x1_ready, 1)
                elif kind == "ln" and i[0] == 0:
                    dve.wait_ge(x1_ready, gi + 1)
                    centre(g1[:], g1[:], TPC)
                elif kind == "ln" and i[0] == 1:
                    variance(g1[:], g2[:], TPC, 1e-5)
                elif kind == "ln":
                    inv_sqrt(TPC, roots.next(w, gi))
                    v.tensor_tensor(g1[:], g1[:], spread(3, TPC), ALU.mult).then_inc(xn_ready, 1)
                elif kind == "gQ":
                    dve.wait_ge(ring_full[k], turn + 1)
                    v.tensor_scalar(Q32[:], PS[:, 5 + k, 0:TC], bias[:, 0:1], None, ALU.add).then_inc(q32_ready, 1)
                elif kind == "sp" and i[0] == 0:
                    dve.wait_ge(q32_ready, gi + 1)
                    chain(v.tensor_copy(qpart[:, 0, :], Q32[:]))
                    chain(v.tensor_tensor(Q32[:], Q32[:], qpart[:, 0, :], ALU.subtract))
                elif kind == "sp":
                    chain(v.tensor_copy(qpart[:, 1, :], Q32[:]))
                    v.tensor_tensor(qpart[:, 2, :], Q32[:], qpart[:, 1, :], ALU.subtract).then_inc(qcat_src, 1)

            ring = Ring()

            def step(b, w, gi, slots):
                for kind, i in [item for slot in slots for item in slot]:
                    k, turn = ring.next() if kind in RINGED else (None, None)
                    bk = PS[:, 5 + k, :] if kind in RINGED else None
                    if kind in ("m", "M", "O", "A"):
                        dve.wait_ge(ring_full[k], turn + 1)
                    if kind == "Z":
                        if w >= 1:
                            dve.wait_ge(scores_ready, b * KT)
                        if (w + 1) % LOOP == 0:
                            dve.wait_ge(qcat_in, (gi + 1) * (16 * CMB))
                        at = (w + 1) % LOOP * S
                        for h in range(2):
                            ins = v.tensor_scalar(Qs[0:SR, (w + 1) % 2, :, h, :], Qcat[:, :, at:at + S],
                                                  head_mask[:, h:h + 1], None, ALU.mult)
                            if h == 0:
                                chain.mark(ins)
                            else:
                                ins.then_inc(q_ready, 1)
                    elif kind == "E":
                        dve.wait_ge(pv_done, b * KT)
                        v.tensor_copy(osb[:, :, 0:S], PS[:, 4, 0:2 * PC].rearrange("p (a q) -> p a q", q=S)
                                      ).then_inc(o_copied, 1)
                    elif kind == "m":
                        g, j = i
                        v.tensor_reduce(mthird[:, j, g:g + 1], bk[0:PC, 0:GK], AX.X, ALU.max).then_inc(max_taken, 1)
                        if g == G - 1 and j == NJ - 1:
                            dve.wait_ge(max_taken, (b + 2) * (G * NJ))
                            v.tensor_reduce(mrow[:], mthird[:], AX.X, ALU.max).then_inc(max_ready, 1)
                    elif kind == "M":
                        if w >= 0:
                            dve.wait_ge(shift_in, (b + 1) * 32)
                        chain(v.tensor_scalar(shift[:, 0, :], bk[0:NJ, 0:PC], -1.0, None, ALU.mult))
                        v.scalar_tensor_tensor(out=shift[:, 1, :], in0=bk[0:NJ, 0:PC], scalar=-1.0,
                                               in1=shift[:, 0, :], op0=ALU.mult, op1=ALU.subtract).then_inc(shift_ready, 1)
                    elif kind == "O":
                        to = attn[0:S, :].rearrange("q (r c i d) -> q r c i d", r=2, c=4, i=2)
                        for h in range(2):
                            pv = bk[64 * h:64 * h + S, 0:256].rearrange("q (r c e) -> q r c e", r=2, e=32)
                            chain(v.reciprocal(rsum[:, 2 * h:2 * h + 2, :], pv[:, :, :, PR]))
                            ins = v.tensor_tensor(to[:, :, :, h, :], pv[:, :, :, h * HD:(h + 1) * HD],
                                                  rsum[:, 2 * h:2 * h + 2, :].unsqueeze(3).broadcast_to([S, 2, 4, HD]),
                                                  ALU.mult)
                            if h == 0:
                                chain.mark(ins)
                            else:
                                ins.then_inc(attn_ready, 1)
                    elif kind == "A":
                        v.tensor_scalar(attnT[:, bass.ds((b - 1) * S, S)], bk[:, 0:S], bias[:, 2:3], None, ALU.add
                                        ).then_inc(attnT_ready, 1)
                    elif kind == "Y":
                        dve.wait_ge(ring_full[k], turn + 1)
                        tiles = slice(i[0] * TPC, (i[0] + 1) * TPC)
                        v.tensor_tensor(X[:, tiles, :], bk[0:P].rearrange("p (t d) -> p t d", d=D), X[:, tiles, :], ALU.add
                                        ).then_inc(x2_ready, 1)
                        dve.wait_ge(x2_ready, i[0] + 1)
                        chain(v.tensor_reduce(small[:, 2, tiles], X[:, tiles, :], AX.X, ALU.add))
                        chain(v.tensor_scalar(small[:, 2, tiles], small[:, 2, tiles], 1.0 / D, None, ALU.mult))
                        chain(v.tensor_tensor(N1[:, tiles, :], X[:, tiles, :],
                                              small[:, 2, tiles].unsqueeze(2).broadcast_to([P, TPC, D]), ALU.subtract))
                        chain(v.tensor_tensor(g2[:], N1[:, tiles, :], N1[:, tiles, :], ALU.mult))
                        chain(v.tensor_reduce(small[:, 2, tiles], g2[:], AX.X, ALU.add))
                        ins = v.tensor_scalar(small[:, 0, tiles], small[:, 2, tiles], 1.0 / D, 1e-5, ALU.mult, ALU.add)
                        if i[0] == NC - 1:
                            ins.then_inc(var_ready, 1)
                    else:
                        group_item(kind, i, w, gi, k, turn)

            walk(dve, ring, step, chain, DVE_STEPS)

            inv_sqrt(NT, START_ROOTS + 2 * ROUNDS + 1)
            for c in range(NC):
                tiles = slice(c * TPC, (c + 1) * TPC)
                v.tensor_tensor(N1[:, tiles, :], N1[:, tiles, :],
                                small[:, 3, tiles].unsqueeze(2).broadcast_to([P, TPC, D]), ALU.mult).then_inc(zn_ready, 1)
            v.memset(tmp[:, 0, 0:1], 0.0).then_inc(h_ready, 2)
            v.memset(tmp[:, 0, 1:2], 0.0).then_inc(acc_ready, 2)
            dve.wait_ge(rT_mm, 1)
            v.tensor_copy(rT[:], PS[:, 7, 0:E]).then_inc(rT_ready, 1)

            def per_token(k):
                return small[:, k, :].unsqueeze(2).broadcast_to([P, NT, E])

            dve.wait_ge(logit_mm, 1)
            logits = PS[0:P, 6, 0:NT * E].rearrange("p (t e) -> p t e", e=E)
            chain(v.tensor_reduce(small[:, 7, :], logits, AX.X, ALU.max))
            v.tensor_tensor(lt[0][:], logits, per_token(7), ALU.subtract).then_inc(logit_sub, 1)
            dve.wait_ge(logit_exp, 1)
            chain(v.tensor_reduce(small[:, 8, :], lg[:], AX.X, ALU.add))
            chain(v.reciprocal(small[:, 8, :], small[:, 8, :]))
            chain(v.tensor_tensor(lg[:], lg[:], per_token(8), ALU.mult))
            ranks = rank[:].unsqueeze(1).broadcast_to([P, NT, E])
            for best in range(2):
                src, hit, sel = lg if best == 0 else lt[3], lt[1], lt[2 + 2 * best]
                chain(v.tensor_reduce(small[:, 9 + best, :], src[:], AX.X, ALU.max))
                chain(v.tensor_tensor(hit[:], src[:], per_token(9 + best), ALU.is_equal))
                chain(v.tensor_tensor(hit[:], hit[:], ranks, ALU.mult))
                chain(v.tensor_reduce(small[:, 11, :], hit[:], AX.X, ALU.max))
                chain(v.tensor_tensor(sel[:], ranks, per_token(11), ALU.is_equal))
                if best == 0:
                    chain(v.scalar_tensor_tensor(out=lt[3][:], in0=sel[:], scalar=-2.0, in1=lg[:],
                                                 op0=ALU.mult, op1=ALU.add))
                chain(v.tensor_tensor(sel[:], sel[:], per_token(9 + best), ALU.mult))
            chain(v.tensor_tensor(small[:, 12, :], small[:, 9, :], small[:, 10, :], ALU.add))
            chain(v.reciprocal(small[:, 12, :], small[:, 12, :]))
            chain(v.tensor_tensor(lt[5][:], lt[2][:], lt[4][:], ALU.add))
            chain(v.tensor_tensor(lt[5][:], lt[5][:], per_token(12), ALU.mult))
            dve.wait_ge(acc_ready, 2)
            with dve.Fori(0, E // 2) as it:
                chain.enter(it, 2 * NC)
                for u in range(2):
                    e = it * 2 + u

                    def accumulate(m):
                        dve.wait_ge(down_mm, e * NC + (m + 1))
                        weight = lt[5][:, m * TPC:(m + 1) * TPC, bass.ds(e, 1)].broadcast_to([P, TPC, D])
                        chain(v.tensor_tensor(tmp[:], PS[0:P, 4 + m % 2, :].rearrange("p (t d) -> p t d", d=D),
                                              weight, ALU.mult))
                        rows = X[:, m * TPC:(m + 1) * TPC, :]
                        v.tensor_tensor(rows, rows, tmp[:], ALU.add).then_inc(acc_ready, 1)

                    for m in range(NC):
                        for f in range(FT):
                            k = m * FT + f
                            dve.wait_ge(silu_ready, e * (NC * FT) + (k + 1))
                            dve.wait_ge(gu_mm, e * (NC * FT) + (k + 1))
                            v.tensor_tensor(hT[:, m % 2, f, :], sg[:, k % 2], PS[0:FP, 2 + k % 2, 0:TC], ALU.mult
                                            ).then_inc(h_ready, 1)
                            if f == 2 and m > 0:
                                accumulate(m - 1)
                    accumulate(NC - 1)
                chain.leave(E // 2)


def kernel(x, ctx_1024, mask_BxS2_bk0, L0_attn_wq, L0_attn_wk, L0_attn_wv, L0_attn_wo, L0_xattn_Wq, L0_xattn_bq,
           L0_xattn_Wkv, L0_xattn_bkv, L0_xattn_Wo, L0_xattn_bo, L0_ffn_router_w, L0_ffn_w_gate, L0_ffn_w_up,
           L0_ffn_w_down):
    import numpy as np
    import concourse.bacc as bacc
    from concourse.bass_utils import run_bass_kernel_spmd

    def by_row(w):
        return w.reshape(w.shape[0], NJ, PR).transpose(0, 2, 1).reshape(w.shape[0], D)

    f = np.asarray
    kv = f(L0_xattn_Wkv)
    bkv = f(L0_xattn_bkv)
    arrays = {
        "x": f(x), "ctx": f(ctx_1024), "mask": f(mask_BxS2_bk0),
        "wqkvo": np.stack([f(L0_attn_wq), f(L0_attn_wk), f(L0_attn_wv), f(L0_attn_wo)]),
        "xWq": by_row(f(L0_xattn_Wq)), "xbq": by_row(f(L0_xattn_bq)[None]).T,
        "xWk": by_row(kv[:, :D]), "xbk": by_row(bkv[None, :D]).T,
        "xWv": kv[:, D:], "xbv": bkv[D:, None],
        "xWo": f(L0_xattn_Wo), "xbo": f(L0_xattn_bo)[None],
        "router": f(L0_ffn_router_w), "w_gate": f(L0_ffn_w_gate), "w_up": f(L0_ffn_w_up), "w_down": f(L0_ffn_w_down),
        "ident": np.eye(128, dtype=np.float32),
        "head_rows": ((np.arange(SR)[:, None] // HD) % 2 == np.arange(2)[None]).astype(np.float32),
        "expert_rank": np.arange(E, 0, -1).astype(np.float32)[None],
    }
    arrays = {k: np.ascontiguousarray(v) for k, v in arrays.items()}
    nc = bacc.Bacc("TRN2", target_bir_lowering=False, num_devices=1)
    args = {k: nc.dram_tensor(k, v.shape, mybir.dt.from_np(v.dtype), kind="ExternalInput").ap()
            for k, v in arrays.items()}
    out = nc.dram_tensor("out", (B, S, D), F32, kind="ExternalOutput").ap()
    decoder_kernel(nc, out=out, **args)
    r = run_bass_kernel_spmd(nc, [arrays], core_ids=[0])
    return r.results[0]["out"]
```
